# Optimizing a Trainium2 kernel written in Bass

```python
import numpy as np
import jax
import jax.numpy as jnp

def _softmax(x, axis=-1):
    return jax.nn.softmax(x, axis=axis)

def _gelu(x):
    return jax.nn.gelu(x, approximate=True)

def _silu(x):
    return jax.nn.silu(x)

def _sigmoid(x):
    return jax.nn.sigmoid(x)

def _layernorm(x, axis=-1, eps=1e-05):
    m = jnp.mean(x, axis=axis, keepdims=True)
    v = jnp.var(x, axis=axis, keepdims=True)
    return (x - m) / jnp.sqrt(v + eps)

def _scatter_add(tgt, idx, src, axis=0):
    return tgt.at[idx].add(src)

def _segment_sum(src, seg, n):
    return jax.ops.segment_sum(src, seg, n)
kernel_name = 'mk_adj_resnorm_d4_adj_r2_ce3f48'

def setup_inputs(seed: int=0):
    np.random.seed(seed)
    _w = jnp.asarray

    def _rec_inputs():
        import jax
        import jax.numpy as jnp
        _gk = jax.random.key(seed)
        x = 0.0001732 + 1 * jax.random.normal(jax.random.fold_in(_gk, 1), (5120, 64), jnp.float32)
        _a = jax.random.bernoulli(jax.random.fold_in(_gk, 2), 0.00078125, (5120, 5120))
        _af = _a.astype(jnp.float32)
        _af = _af * jax.random.uniform(jax.random.fold_in(_gk, 3), (5120, 5120), jnp.float32, 0.05, 0.02)
        adj = _af
        return (x, adj)
    x, adj = _rec_inputs()

    def _L0_gnn_setup():
        import jax, jax.numpy as jnp
        import numpy as np
        N_USERS = 2048
        N_ITEMS = 3072
        EMB = 64
        LN_EPS = 1e-05
        key = jax.random.key(seed)
        ks = jax.random.split(key, 10)
        N = N_USERS + N_ITEMS
        ego = jax.random.normal(ks[0], (N, EMB), jnp.float32)
        adj = (jax.random.uniform(ks[1], (N, N), jnp.float32) < 0.01).astype(jnp.float32) * 0.02
        xav = float(np.sqrt(6.0 / (EMB + EMB)))
        W_u = jax.random.uniform(ks[2], (EMB, EMB), jnp.float32, -xav, xav)
        W_i = jax.random.uniform(ks[3], (EMB, EMB), jnp.float32, -xav, xav)
        diag_u = jax.random.uniform(ks[4], (N_USERS,), jnp.float32, 0.99, 1.01)
        diag_i = jax.random.uniform(ks[5], (N_ITEMS,), jnp.float32, 0.99, 1.01)
        par_u = jax.random.uniform(ks[6], (2,), jnp.float32, 0.0, 0.99)
        par_i = jax.random.uniform(ks[7], (2,), jnp.float32, 0.0, 0.99)
        ln_gamma = jnp.ones((EMB,), jnp.float32)
        ln_beta = jnp.zeros((EMB,), jnp.float32)
        return {'ego_embeddings': ego, 'adj': adj, 'W_u': W_u, 'diag_u': diag_u, 'par_u': par_u, 'W_i': W_i, 'diag_i': diag_i, 'par_i': par_i, 'ln_gamma': ln_gamma, 'ln_beta': ln_beta}
    _L0_gnn_all = _L0_gnn_setup()
    _L0_gnn_in = {k: v for k, v in _L0_gnn_all.items() if k in ('W_u', 'diag_u', 'par_u', 'W_i', 'diag_i', 'par_i', 'ln_gamma', 'ln_beta')}
    del _L0_gnn_all

    def _L1_gnn_setup():
        import jax, jax.numpy as jnp
        import numpy as np
        F_CONST = 1.0
        B_CONST = 0.1
        R_CONST = 0.01
        N, DIM = (4096, 64)
        key = jax.random.key(seed)
        k1, k2 = jax.random.split(key)
        x = jax.random.uniform(k1, (N, DIM), dtype=jnp.float32)
        A = jax.random.uniform(k2, (N, N), dtype=jnp.float32)
        return {'t': 0, 'x': x, 'A': A}
    _L1_gnn_all = _L1_gnn_setup()
    _L1_gnn_in = {k: v for k, v in _L1_gnn_all.items() if k in ()}
    del _L1_gnn_all

    def _L2_gnn_setup():
        import jax, jax.numpy as jnp
        import numpy as np
        N, D_IN, D_OUT = (8192, 64, 64)
        AVG_DEG = 32.0
        L2_EPS = 1e-12
        key = jax.random.key(seed)
        kx, ka, kw, kb = jax.random.split(key, 4)
        X = jax.random.normal(kx, (N, D_IN), dtype=jnp.float32)
        adj = (jax.random.uniform(ka, (N, N)) < AVG_DEG / N).astype(jnp.float32)
        bound = 1.0 / np.sqrt(2 * D_IN)
        W = jax.random.uniform(kw, (2 * D_IN, D_OUT), dtype=jnp.float32, minval=-bound, maxval=bound)
        b = jax.random.uniform(kb, (D_OUT,), dtype=jnp.float32, minval=-bound, maxval=bound)
        return {'X': X, 'adj': adj, 'W': W, 'b': b}
    _L2_gnn_all = _L2_gnn_setup()
    _L2_gnn_in = {k: v for k, v in _L2_gnn_all.items() if k in ('W', 'b')}
    del _L2_gnn_all

    def _L3_gnn_setup():
        import jax, jax.numpy as jnp
        import numpy as np
        N, IN_F, OUT_F, K = (8192, 64, 64, 4)
        key = jax.random.key(seed)
        k1, k2, k3 = jax.random.split(key, 3)
        x = jax.random.normal(k1, (N, IN_F), dtype=jnp.float32)
        L_scaled = jax.random.normal(k2, (N, N), dtype=jnp.float32) / np.sqrt(N)
        fan_in, fan_out = (K * IN_F, OUT_F)
        bound = np.sqrt(6.0 / (fan_in + fan_out))
        weight = jax.random.uniform(k3, (K, IN_F, OUT_F), dtype=jnp.float32, minval=-bound, maxval=bound)
        bias = jnp.zeros((OUT_F,), dtype=jnp.float32)
        return {'x': x, 'L_scaled': L_scaled, 'weight': weight, 'bias': bias}
    _L3_gnn_all = _L3_gnn_setup()
    _L3_gnn_in = {k: v for k, v in _L3_gnn_all.items() if k in ('weight', 'bias')}
    del _L3_gnn_all
    return {'x': x, 'adj': adj, 'L0_gnn_W_u': _L0_gnn_in['W_u'], 'L0_gnn_diag_u': _L0_gnn_in['diag_u'], 'L0_gnn_par_u': _L0_gnn_in['par_u'], 'L0_gnn_W_i': _L0_gnn_in['W_i'], 'L0_gnn_diag_i': _L0_gnn_in['diag_i'], 'L0_gnn_par_i': _L0_gnn_in['par_i'], 'L0_gnn_ln_gamma': _L0_gnn_in['ln_gamma'], 'L0_gnn_ln_beta': _L0_gnn_in['ln_beta'], 'L2_gnn_W': _L2_gnn_in['W'], 'L2_gnn_b': _L2_gnn_in['b'], 'L3_gnn_weight': _L3_gnn_in['weight'], 'L3_gnn_bias': _L3_gnn_in['bias']}

def reference(x, adj, L0_gnn_W_u, L0_gnn_diag_u, L0_gnn_par_u, L0_gnn_W_i, L0_gnn_diag_i, L0_gnn_par_i, L0_gnn_ln_gamma, L0_gnn_ln_beta, L2_gnn_W, L2_gnn_b, L3_gnn_weight, L3_gnn_bias):
    import jax
    import jax.numpy as jnp

    def _L0_gnn_ref(ego_embeddings, adj, W_u, diag_u, par_u, W_i, diag_i, par_i, ln_gamma, ln_beta):
        import jax, jax.numpy as jnp
        import numpy as np
        N_USERS = 2048
        N_ITEMS = 3072
        EMB = 64
        LN_EPS = 1e-05
        nu = diag_u.shape[0]
        res = ego_embeddings
        ego_u = ego_embeddings[:nu]
        ego_i = ego_embeddings[nu:]
        u = par_u[0] * par_u[1] * (diag_u[:, None] * ego_u @ W_u) + ego_u
        i = par_i[0] * par_i[1] * (diag_i[:, None] * ego_i @ W_i) + ego_i
        e = jnp.concatenate([u, i], axis=0)
        h = adj @ (adj.T @ e)
        mu = jnp.mean(h, axis=-1, keepdims=True)
        var = jnp.var(h, axis=-1, keepdims=True)
        out = (h - mu) * jax.lax.rsqrt(var + LN_EPS) * ln_gamma + ln_beta + res
        return out

    def _L1_gnn_ref(t, x, A):
        import jax, jax.numpy as jnp
        import numpy as np
        F_CONST = 1.0
        B_CONST = 0.1
        R_CONST = 0.01
        N, DIM = (4096, 64)
        Ax = A @ x
        outer = R_CONST * jnp.sum(x * Ax, axis=1, keepdims=True)
        return F_CONST - B_CONST * x - outer

    def _L2_gnn_ref(X, adj, W, b):
        import jax, jax.numpy as jnp
        import numpy as np
        N, D_IN, D_OUT = (8192, 64, 64)
        AVG_DEG = 32.0
        L2_EPS = 1e-12
        deg = jnp.clip(jnp.sum(adj, axis=1, keepdims=True) + 1.0, 1.0, None)
        h_neigh = (adj @ X + X) / deg
        concat = jnp.concatenate([X, h_neigh], axis=1)
        z = concat @ W + b
        out = jax.nn.relu(z)
        norm = jnp.linalg.norm(out, axis=1, keepdims=True)
        return out / jnp.maximum(norm, L2_EPS)

    def _L3_gnn_ref(x, L_scaled, weight, bias):
        import jax, jax.numpy as jnp
        import numpy as np
        N, IN_F, OUT_F, K = (8192, 64, 64, 4)
        Tx_prev2 = x
        Tx_prev1 = L_scaled @ x
        out = Tx_prev2 @ weight[0]
        if K > 1:
            out = out + Tx_prev1 @ weight[1]
        for k in range(2, K):
            Tx_curr = 2.0 * (L_scaled @ Tx_prev1) - Tx_prev2
            out = out + Tx_curr @ weight[k]
            Tx_prev2, Tx_prev1 = (Tx_prev1, Tx_curr)
        return out + bias
    x = _layernorm(x + _L0_gnn_ref(x, adj, L0_gnn_W_u, L0_gnn_diag_u, L0_gnn_par_u, L0_gnn_W_i, L0_gnn_diag_i, L0_gnn_par_i, L0_gnn_ln_gamma, L0_gnn_ln_beta), axis=-1)
    x = _layernorm(x + _L1_gnn_ref(0, x, adj), axis=-1)
    x = _layernorm(x + _L2_gnn_ref(x, adj, L2_gnn_W, L2_gnn_b), axis=-1)
    x = _layernorm(x + _L3_gnn_ref(x, adj, L3_gnn_weight, L3_gnn_bias), axis=-1)
    return x

_drawn_inputs = setup_inputs


def setup_inputs(seed=0):
    import zlib

    import numpy as np

    out = dict(_drawn_inputs(seed))
    spreads = {'L0_gnn_ln_gamma': (1.0, 0.2), 'L0_gnn_ln_beta': (0.0, 0.1), 'L3_gnn_bias': (0.0, 0.1)}
    factors = {'L0_gnn_diag_u': 8.0, 'L0_gnn_W_i': 6.447, 'L0_gnn_diag_i': 8.0, 'L2_gnn_b': 4.502}
    for name, (base, spread) in spreads.items():
        noise = np.random.default_rng([zlib.crc32(name.encode()), seed]).standard_normal(out[name].shape)
        drawn = base * np.exp(spread * noise) if base else spread * noise
        out[name] = jnp.asarray(drawn.astype(out[name].dtype))
    for name, factor in factors.items():
        out[name] = (out[name] * factor).astype(out[name].dtype)
    return out
```

```python
from contextlib import ExitStack

import concourse.bass as bass
from concourse import mybir

F32 = mybir.dt.float32
F32R = mybir.dt.float32r
ALU = mybir.AluOpType
ACT = mybir.ActivationFunctionType
AX = mybir.AxisListType

P = 128
LN_EPS = 1e-5
L2_EPS = 1e-12


def build(nc, x, adj, w_u, diag_u, par_u, w_i, diag_i, par_i, gamma, beta, l2_w, l2_b, l3_w, l3_b, out):
    N, F = x.shape
    BLK = 512
    NB = N // BLK
    TB = BLK // P
    NT = N // P
    UB = diag_u.shape[0] // BLK
    UT = UB * TB
    HT = TB // 2
    NAT = 5
    BLOCKS = NB * NB
    assert NB % NAT == 0 and NB % 2 == 0

    at_dram = nc.dram_tensor("a_transposed", [NB, NB, P, TB * BLK], F32, kind="Internal").ap()
    a_blocks = adj.rearrange("(t p) j -> p t j", p=P)
    x_rows = x.rearrange("(t p) f -> p t f", p=P)
    out_rows = out.rearrange("(t p) f -> p t f", p=P)

    ctx = ExitStack()
    with ctx:
        def sb(name, shape, dt=F32):
            return ctx.enter_context(nc.sbuf_tensor(name, shape, dt))

        def pb(name):
            return ctx.enter_context(nc.psum_tensor(name, [P, BLK], F32))

        def sem(name):
            return ctx.enter_context(nc.semaphore(name))

        at_raw = sb("at_raw", [P, NB, TB, BLK])
        at_hi = sb("at_hi", [P, 2 * 2, HT, BLK], F32R)
        at_lo = sb("at_lo", [P, 2 * 2, HT, BLK], F32R)
        rows = sb("rows", [P, NT, F])
        h_sum = sb("h_sum", [P, N])
        l3_sum = h_sum[:, 0:NT * F].rearrange("p (t f) -> p t f", t=NT)
        row_part = sb("row_part", [P, NT, NB])
        inv_deg = sb("inv_deg", [P, NT])
        u_split = sb("u_split", [P, TB, 2, F], F32R)
        y_turned = sb("y_turned", [P, BLK])
        x_turned = sb("x_turned", [F, BLK])
        x_block = sb("x_block", [P, TB, F])
        ta, tb_, tc, td = (sb(f"temp{k}", [P, TB, F]) for k in range(4))
        stat = sb("stat", [P, 4, TB])
        ident = sb("ident", [P, P])
        ident2 = sb("ident2", [P, F])
        w0 = sb("w0", [F, 2, F])
        w2x = sb("w2x", [F, 2, F])
        w3x = sb("w3x", [F, 2, F])
        twice = sb("twice", [P, 4, F])
        diag_flat = sb("diag_flat", [NT, P])
        diag = sb("diag", [P, NT])
        par = sb("par", [P, 2, 2])
        par_prod = sb("par_prod", [P, 2])
        vec = sb("vec", [P, 4, F])
        minus_half = sb("minus_half", [P, TB])

        with nc.sbuf_tensor("nat", [P, NAT, TB, BLK], F32) as nat:
            pass
        xs = [sb(f"xs{k}", [P, NT, 2, F], F32R) for k in range(2)]

        ps_t = [pb(f"ps_turn{k}") for k in range(TB)]
        ps_u = pb("ps_u")
        ps_h = [pb(f"ps_h{k}") for k in range(2)]
        ps_back = pb("ps_back")
        back = ps_back[:, 0:TB * F].rearrange("p (t f) -> p t f", t=TB)
        ps_y = ps_u
        yw = [ps_t[0][:, 0:TB * F].rearrange("p (t f) -> p t f", t=TB),
              ps_t[1][:, 0:TB * F].rearrange("p (t f) -> p t f", t=TB),
              ps_t[2][:, 0:TB * F].rearrange("p (t f) -> p t f", t=TB)]
        ps_xt = ps_h[0]
        xw = ps_h[1][:, :].rearrange("p (t w f) -> p t w f", t=TB, w=2)

        consts_loaded = sem("consts_loaded")
        x_loaded = sem("x_loaded")
        x_reloaded = sem("x_reloaded")
        ident_ready = sem("ident_ready")
        diag_turned = sem("diag_turned")
        xt_ready = sem("xt_ready")
        xt_copied = sem("xt_copied")
        xw_ready = sem("xw_ready")
        xw_used = sem("xw_used")
        nat_loaded = [sem(f"nat_loaded{k}") for k in range(NAT)]
        nat_summed = sem("nat_summed")
        u_added = sem("u_added")
        u_copied = sem("u_copied")
        u_back = sem("u_back")
        u_ready = sem("u_ready")
        turned = sem("turned")
        at_evacuated = sem("at_evacuated")
        at_stored = [sem(f"at_stored{k}") for k in range(NB)]
        hi_ready = sem("hi_ready")
        lo_ready = sem("lo_ready")
        multiplied = sem("multiplied")
        h_free = sem("h_free")
        hy_ready = sem("hy_ready")
        raw_loaded = [sem(f"raw_loaded{k}") for k in range(NB)]
        x_block_ready = sem("x_block_ready")
        y_copied = sem("y_copied")
        y_back = sem("y_back")
        y_used = sem("y_used")
        var_ready = sem("var_ready")
        pow_ready = sem("pow_ready")
        rows_ready = sem("rows_ready")
        out_ready = sem("out_ready")
        stored = sem("stored")

        block = ctx.enter_context(nc.Block())
        N_CONSTS = 22
        N_ROOTS = 6 * NB
        X_TIMES = (1, 2)

        @block.sync
        def _(sp):
            sp.dma_start(rows[:, :, :], x_rows).then_inc(x_loaded, 16)

            def load(j, i):
                n = NB * j + i
                if not (isinstance(j, int) and j == 0 and i < NAT):
                    sp.wait_ge(u_added, n - NAT + 1)
                    sp.wait_ge(nat_summed, n - NAT + 1)
                sp.dma_start(nat[:, i % NAT], a_blocks[:, i * TB:(i + 1) * TB, bass.ds(j * BLK, BLK)])\
                    .then_inc(nat_loaded[i % NAT], 16)

            for i in range(NB):
                load(0, i)
            with sp.Fori(1, NB) as j:
                for i in range(NB):
                    load(j, i)
            sp.wait_ge(u_added, BLOCKS)
            sp.dma_start(rows[:, :, :], x_rows).then_inc(x_reloaded, 16)
            for s in at_stored:
                sp.wait_ge(s, 16 * NB)
            for k in range(5):
                with sp.Fori(0, NB) as i:
                    for j in range(NB):
                        sp.wait_ge(lo_ready, 2 * (BLOCKS * k + NB * i + j + BLOCKS - NB + 1))
                        sp.dma_start(at_raw[:, j], at_dram[bass.ds(i, 1), j].rearrange("o p n -> p (o n)")
                                     .rearrange("p (t n) -> p t n", t=TB)).then_inc(raw_loaded[j], 16)
            with sp.Fori(0, NB) as i:
                sp.wait_ge(out_ready, i + 1)
                sp.dma_start(out_rows[:, bass.ds(i * TB, TB), :], rows[:, bass.ds(i * TB, TB), :])\
                    .then_inc(stored, 16)
            sp.wait_ge(stored, 16 * NB)

        @block.gpsimd
        def _(pool):
            nc.gpsimd.memset(ident[:, :], 0.0).then_inc(ident_ready, 1)
            pool.wait_ge(ident_ready, 1)
            nc.gpsimd.affine_select(out=ident[:, :], in_=ident[:, :], compare_op=ALU.not_equal, fill=1.0,
                                    base=0, pattern=[[-1, P]], channel_multiplier=1).then_inc(ident_ready, 1)

            def inverse_root(n):
                pool.wait_ge(var_ready, n)
                nc.gpsimd.tensor_tensor(stat[:, 2, :], stat[:, 1, :], minus_half[:, :], ALU.pow)\
                    .then_inc(pow_ready, 1)

            with pool.Fori(0, N_ROOTS) as n:
                inverse_root(n + 1)

        @block.scalar
        def _(act):
            def const(dst, src):
                act.dma_start(dst, src).then_inc(consts_loaded, 16)

            const(diag_flat[0:UT, :], diag_u.rearrange("(t p) -> t p", p=P))
            const(diag_flat[UT:NT, :], diag_i.rearrange("(t p) -> t p", p=P))
            const(par[:, 0, :], par_u.partition_broadcast(P))
            const(par[:, 1, :], par_i.partition_broadcast(P))
            const(w0[:, 0, :], w_u)
            const(w0[:, 1, :], w_i)
            for k, v in enumerate((gamma, beta, l2_b, l3_b)):
                const(vec[:, k, :], v.partition_broadcast(P))
            const(w2x[:, 0, :], l2_w[0:F, :])
            const(w2x[:, 1, :], l2_w[F:2 * F, :])
            const(w3x[:, 0, :], l3_w[0])
            const(w3x[:, 1, :], l3_w[2])
            for h in range(2):
                half = slice(h * F, (h + 1) * F)
                const(twice[half, 0, :], l2_w[F:2 * F, :])
                for k in range(1, 4):
                    const(twice[half, k, :], l3_w[k])

            def split_hi(m, raw):
                for h in range(2):
                    act.wait_ge(multiplied, 2 * m + h + 1)
                    nc.scalar.activation(at_hi[:, 2 * (raw % 2) + h], at_raw[:, raw, h * HT:(h + 1) * HT],
                                         ACT.Copy).then_inc(hi_ready, 1)

            def store(j, i):
                act.wait_ge(at_evacuated, TB * (NB * j + i + 1))
                act.dma_start(at_dram[i, bass.ds(j, 1)].rearrange("o p n -> p (o n)"),
                              at_raw[:, i].rearrange("p t n -> p (t n)")).then_inc(at_stored[i], 16)

            def column(j, first):
                for i in range(NB):
                    if not first:
                        act.wait_ge(at_evacuated, TB * (NB * (j - 1) + i + 1))
                        split_hi(NB * (j - 1) + i, i)
                    if i > 0:
                        store(j, i - 1)
                    if not first:
                        act.wait_ge(lo_ready, 2 * (NB * (j - 1) + i + 1))
                        act.wait_ge(at_stored[i], 16 * j)
                    for t in range(TB):
                        act.wait_ge(turned, TB * (NB * j + i) + t + 1)
                        nc.scalar.activation(at_raw[:, i, t, :], ps_t[t][:, :], ACT.Copy)\
                            .then_inc(at_evacuated, 1)
                store(j, NB - 1)

            column(0, True)
            with act.Fori(1, NB) as j:
                column(j, False)
            for i in range(NB):
                act.wait_ge(at_evacuated, TB * (BLOCKS - NB + i + 1))
                split_hi(BLOCKS - NB + i, i)

            for k in range(5):
                with act.Fori(0, NB) as i:
                    for j in range(NB):
                        act.wait_ge(raw_loaded[j], 16 * NB * k + 16 * i + 16)
                        split_hi(BLOCKS * (k + 1) + NB * i + j, j)
                    act.wait_ge(y_back, NB * k + i + NB)
                    act.wait_ge(multiplied, 2 * (BLOCKS * (k + 1) + NB * (i + 1)) + 4)
                    nc.scalar.activation(y_turned[:, :], ps_y[:, :], ACT.Copy).then_inc(y_copied, 1)

        @block.tensor
        def _(pe):
            pe.sem_inc(multiplied, 4)
            pe.wait_ge(ident_ready, 2)
            pe.wait_ge(consts_loaded, 16 * N_CONSTS)
            pe.matmul(ps_back[:, 0:NT], diag_flat[:, :], ident[0:NT, 0:NT], start=True, stop=True)\
                .then_inc(diag_turned, 1)
            pe.wait_ge(x_loaded, 16)

            def turn_x(i):
                if i > 0:
                    pe.wait_ge(xt_copied, i)
                for t in range(TB):
                    mm = pe.transpose(ps_xt[0:F, t * P:(t + 1) * P], rows[:, i * TB + t, :], ident[:, :])
                mm.then_inc(xt_ready, 1)

            def times_w(i):
                pe.wait_ge(xt_copied, i + 1)
                if i > 0:
                    pe.wait_ge(xw_used, i)
                for t in range(TB):
                    mm = pe.matmul(xw[:, t, 0, :], x_turned[:, t * P:(t + 1) * P], w0[:, int(i >= UB), :],
                                   start=True, stop=True)
                mm.then_inc(xw_ready, 1)

            def multiply(m, slot, left, acc, start, stop):
                for t in range(TB):
                    if t % HT == 0:
                        pe.wait_ge(lo_ready, 2 * m + t // HT + 1)
                    for half in (at_hi, at_lo):
                        mm = pe.matmul(acc[:, :], left(t), half[:, 2 * slot + t // HT, t % HT, :],
                                       start=start and t == 0 and half is at_hi,
                                       stop=stop and t == TB - 1 and half is at_lo)
                    if t % HT == HT - 1:
                        mm.then_inc(multiplied, 1)

            def h_part(j, i):
                m = NB * j + i
                pe.wait_ge(h_free, m + 1)
                multiply(m, i % 2, lambda t: u_split[:, t].rearrange("p h f -> p (h f)"), ps_h[i % 2], True, True)

            def u_turn_back(j):
                pe.wait_ge(u_copied, j + 1)
                for t in range(TB):
                    mm = pe.matmul(back[:, t, :], y_turned[:, t * P:(t + 1) * P], ident2[:, :],
                                   start=True, stop=True)
                mm.then_inc(u_back, 1)

            def column(j, first):
                for i in range(NB):
                    n = NB * j + i
                    if first and i + 1 < NB:
                        turn_x(i + 1)
                    pe.wait_ge(nat_loaded[i % NAT], 32 * j + 16 * (i // NAT + 1))
                    for t in range(TB):
                        if not (first and i == 0):
                            pe.wait_ge(at_evacuated, TB * (n - 1) + t + 1)
                        for c in range(TB):
                            mm = pe.transpose(ps_t[t][:, c * P:(c + 1) * P],
                                              nat[:, i % NAT, c, t * P:(t + 1) * P], ident[:, :])
                        mm.then_inc(turned, 1)
                    if first:
                        if i + 1 < NB:
                            times_w(i + 1)
                        pe.wait_ge(xw_used, i + 1)
                    elif i == 0:
                        pe.wait_ge(u_copied, j)
                    for c in range(TB):
                        side = slice(c % 2 * F, (c % 2 + 1) * F)
                        mm = pe.matmul(ps_u[side, :], rows[:, i * TB + c, :], nat[:, i % NAT, c, :],
                                       start=i == 0 and c < 2, stop=i == NB - 1 and c >= TB - 2)
                    mm.then_inc(u_added, 1)
                    if not first:
                        if i == 0:
                            u_turn_back(j - 1)
                            pe.wait_ge(u_ready, j)
                        else:
                            h_part(j - 1, i - 1)
                if not first:
                    h_part(j - 1, NB - 1)

            turn_x(0)
            times_w(0)
            column(0, True)
            with pe.Fori(1, NB) as j:
                column(j, False)
            u_turn_back(NB - 1)
            pe.wait_ge(u_ready, NB)

            def turn_back(n, outs):
                pe.wait_ge(y_copied, n + 1)
                for dst, w in outs:
                    for t in range(TB):
                        mm = pe.matmul(dst[:, t, :], y_turned[:, t * P:(t + 1) * P], w, start=True, stop=True)
                mm.then_inc(y_back, 1)

            for i in range(NB):
                h_part(NB - 1, i)
                pe.wait_ge(hy_ready, i + 1)
                if i > 0:
                    pe.wait_ge(y_used, i)
                for t in range(TB):
                    mm = pe.matmul(back[:, t, :], y_turned[:, t * P:(t + 1) * P], ident2[:, :],
                                   start=True, stop=True)
                mm.then_inc(y_back, 1)

            def turn_x_block(n):
                pe.wait_ge(x_block_ready, n + 1)
                for t in range(TB):
                    mm = pe.matmul(ps_xt[0:F, t * P:(t + 1) * P], x_block[:, t, :], ident[:, :],
                                   start=True, stop=True)
                mm.then_inc(xt_ready, 1)

            def x_times(n, w):
                pe.wait_ge(xt_copied, NB + n + 1)
                for t in range(TB):
                    mm = pe.matmul(xw[:, t], x_turned[:, t * P:(t + 1) * P], w[:, :, :], start=True, stop=True)
                mm.then_inc(xw_ready, 1)

            BACK = (((yw[0], ident2[:, :]),),
                    ((yw[1], twice[:, 0, :]),),
                    ((yw[0], ident2[:, :]), (yw[1], twice[:, 1, :]), (yw[2], twice[:, 3, :])),
                    ((yw[0], ident2[:, :]), (yw[1], twice[:, 2, :])),
                    ((yw[0], twice[:, 3, :]),))

            def finish_row_turn(k, n):
                pe.wait_ge(y_used, n + NB)
                turn_back(n, BACK[k])
                if k in X_TIMES:
                    turn_x_block(X_TIMES.index(k) * NB + n - k * NB)

            def finish_row_times(k, n):
                if k in X_TIMES:
                    x_times(X_TIMES.index(k) * NB + n - k * NB, (w2x, w3x)[X_TIMES.index(k)])

            def row(k, i, before):
                for j in range(NB):
                    if j == 0:
                        if not (k == 0 and isinstance(i, int)):
                            pe.wait_ge(y_copied, NB * k + i)
                    pe.wait_ge(rows_ready, NB * k + j + 1)
                    multiply(BLOCKS * (k + 1) + NB * i + j, j % 2,
                                  lambda t: xs[k % 2][:, j * TB + t].rearrange("p h f -> p (h f)"),
                                  ps_y, j == 0, j == NB - 1)
                    if j == 0 and before:
                        finish_row_turn(*before)
                    if j == 2 and before:
                        finish_row_times(*before)

            for k in range(5):
                row(k, 0, (k - 1, NB * k - 1) if k > 0 else None)
                with pe.Fori(1, NB) as i:
                    row(k, i, (k, NB * k + i - 1))
            finish_row_turn(4, 5 * NB - 1)

        @block.vector
        def _(dve):
            V = nc.vector

            def split_rows(src, dst_hi, dst_lo):
                V.tensor_copy(dst_hi, src)
                dve.drain()
                return V.tensor_tensor(dst_lo, src, dst_hi.bitcast(F32), ALU.subtract)

            V.memset(minus_half[:, :], -0.5)
            V.memset(h_sum[:, 0:N // 2], 0.0).then_inc(h_free, 1)
            V.memset(h_sum[:, N // 2:N], 0.0).then_inc(h_free, 1)
            dve.wait_ge(consts_loaded, 16 * N_CONSTS)
            dve.wait_ge(ident_ready, 2)
            V.tensor_tensor(ident2[:, :], ident[:, 0:F], ident[:, F:P], ALU.add)
            V.tensor_tensor(par_prod[:, :], par[:, :, 0], par[:, :, 1], ALU.mult)
            dve.drain()
            dve.wait_ge(diag_turned, 1)
            V.tensor_scalar(diag[:, 0:UT], ps_back[:, 0:UT], par_prod[:, 0:1], None, ALU.mult)
            V.tensor_scalar(diag[:, UT:NT], ps_back[:, UT:NT], par_prod[:, 1:2], None, ALU.mult)
            dve.drain()

            def make_e(i):
                tiles = slice(i * TB, (i + 1) * TB)
                dve.wait_ge(xt_ready, i + 1)
                V.tensor_copy(x_turned[:, :], ps_xt[0:F, :]).then_inc(xt_copied, 1)
                dve.wait_ge(xw_ready, i + 1)
                V.tensor_tensor(ta[:, :, :], xw[:, :, 0, :],
                                diag[:, tiles].unsqueeze(2).broadcast_to([P, TB, F]), ALU.mult)
                dve.drain()
                V.tensor_tensor(rows[:, tiles, :], rows[:, tiles, :], ta[:, :, :], ALU.add).then_inc(xw_used, 1)
                dve.drain()

            def split_lo(m, raw):
                for h in range(2):
                    slot = 2 * (raw % 2) + h
                    dve.wait_ge(hi_ready, 2 * m + h + 1)
                    V.tensor_tensor(at_lo[:, slot], at_raw[:, raw, h * HT:(h + 1) * HT],
                                    at_hi[:, slot].bitcast(F32), ALU.subtract).then_inc(lo_ready, 1)

            def add_h(j, i):
                m = NB * j + i
                dve.wait_ge(multiplied, 2 * m + 6)
                cols = slice(i * BLK, (i + 1) * BLK)
                V.tensor_tensor(h_sum[:, cols], h_sum[:, cols], ps_h[i % 2][:, :], ALU.add).then_inc(h_free, 1)

            def copy_u(j):
                dve.wait_ge(u_added, NB * j + NB)
                V.tensor_copy(y_turned[:, :], ps_u[:, :]).then_inc(u_copied, 1)

            def split_u(j):
                dve.wait_ge(u_back, j + 1)
                split_rows(back, u_split[:, :, 0, :], u_split[:, :, 1, :]).then_inc(u_ready, 1)

            def column(j, first):
                for i in range(NB):
                    if first and i + 1 < NB:
                        make_e(i + 1)
                    if not first:
                        if i == 0:
                            copy_u(j - 1)
                        split_lo(NB * (j - 1) + i, i)
                        if i == 0:
                            split_u(j - 1)
                        else:
                            add_h(j - 1, i - 1)
                    dve.wait_ge(nat_loaded[i % NAT], 32 * j + 16 * (i // NAT + 1))
                    V.reduce_sum(row_part[:, i * TB:(i + 1) * TB, bass.ds(j, 1)].rearrange("p t o -> p (t o)"),
                                 nat[:, i % NAT], AX.X).then_inc(nat_summed, 1)
                if not first:
                    add_h(j - 1, NB - 1)

            make_e(0)
            column(0, True)
            with dve.Fori(1, NB) as j:
                column(j, False)
            copy_u(NB - 1)
            split_lo(BLOCKS - NB, 0)
            split_u(NB - 1)
            dve.drain()
            V.reduce_sum(inv_deg[:, :], row_part[:, :, :], AX.X)
            dve.drain()
            V.tensor_scalar(inv_deg[:, :], inv_deg[:, :], 1.0, 1.0, ALU.add, ALU.max)
            dve.drain()
            V.reciprocal(inv_deg[:, :], inv_deg[:, :])

            roots = [0]

            def to_power(n):
                dve.drain().then_inc(var_ready, 1)
                dve.wait_ge(pow_ready, n)

            def over_rows(s):
                return s.unsqueeze(2).broadcast_to([P, TB, F])

            def norm(src, dst, n):
                V.reduce_sum(stat[:, 0, :], src, AX.X)
                dve.drain()
                V.tensor_scalar(stat[:, 0, :], stat[:, 0, :], 1.0 / F, None, ALU.mult)
                dve.drain()
                V.tensor_tensor(tc[:, :, :], src, over_rows(stat[:, 0, :]), ALU.subtract)
                dve.drain()
                V.tensor_tensor(td[:, :, :], tc[:, :, :], tc[:, :, :], ALU.mult)
                dve.drain()
                V.reduce_sum(stat[:, 3, :], td[:, :, :], AX.X)
                dve.drain()
                V.tensor_scalar(stat[:, 1, :], stat[:, 3, :], 1.0 / F, LN_EPS, ALU.mult, ALU.add)
                to_power(n)
                V.tensor_tensor(dst, tc[:, :, :], over_rows(stat[:, 2, :]), ALU.mult)
                dve.drain()

            def vec_rows(k):
                return vec[:, k, :].unsqueeze(1).broadcast_to([P, TB, F])

            def new_rows(i, k):
                at = bass.ds(i * TB, TB) if not isinstance(i, int) else slice(i * TB, (i + 1) * TB)
                split_rows(rows[:, at, :], xs[k % 2][:, at, 0, :], xs[k % 2][:, at, 1, :])\
                    .then_inc(rows_ready, 1)
                dve.drain()

            dve.wait_ge(x_reloaded, 16)
            for i in range(NB):
                tiles = slice(i * TB, (i + 1) * TB)
                dve.wait_ge(multiplied, 2 * (BLOCKS - NB + i) + 6)
                if i > 0:
                    dve.wait_ge(y_back, i)
                V.tensor_tensor(y_turned[:, :], h_sum[:, i * BLK:(i + 1) * BLK], ps_h[i % 2][:, :], ALU.add)
                dve.drain().then_inc(hy_ready, 1)
                dve.drain().then_inc(h_free, 1)
                if i + 1 < NB:
                    split_lo(BLOCKS - NB + i + 1, i + 1)
                dve.wait_ge(y_back, i + 1)
                norm(back, ta[:, :, :], 2 * i + 1)
                dve.drain().then_inc(y_used, 1)
                V.tensor_tensor(tb_[:, :, :], ta[:, :, :], vec_rows(0), ALU.mult)
                dve.drain()
                V.tensor_tensor(ta[:, :, :], tb_[:, :, :], vec_rows(1), ALU.add)
                dve.drain()
                V.tensor_tensor(tb_[:, :, :], ta[:, :, :], rows[:, tiles, :], ALU.add)
                dve.drain()
                V.tensor_tensor(ta[:, :, :], tb_[:, :, :], rows[:, tiles, :], ALU.add)
                dve.drain()
                norm(ta[:, :, :], rows[:, tiles, :], 2 * i + 2)
                new_rows(i, 0)

            def finish_l1(i, n):
                at = bass.ds(i * TB, TB)
                r = rows[:, at, :]
                V.tensor_tensor(ta[:, :, :], yw[0], r, ALU.mult)
                V.tensor_scalar(tb_[:, :, :], r, 0.9, 1.0, ALU.mult, ALU.add)
                dve.drain().then_inc(y_used, 1)
                V.reduce_sum(stat[:, 0, :], ta[:, :, :], AX.X)
                dve.drain()
                V.tensor_scalar(stat[:, 3, :], stat[:, 0, :], 0.01, None, ALU.mult)
                dve.drain()
                V.tensor_tensor(ta[:, :, :], tb_[:, :, :], over_rows(stat[:, 3, :]), ALU.subtract)
                dve.drain()
                norm(ta[:, :, :], r, 2 * NB + n + 1)
                new_rows(i, 1)

            def copy_x_block(i):
                V.tensor_copy(x_block[:, :, :], rows[:, bass.ds(i * TB, TB), :]).then_inc(x_block_ready, 1)

            def copy_x_turned(n):
                dve.wait_ge(xt_ready, NB + n + 1)
                V.tensor_copy(x_turned[:, :], ps_xt[0:F, :]).then_inc(xt_copied, 1)

            def finish_l2(i, n):
                at = bass.ds(i * TB, TB)
                dve.wait_ge(xw_ready, n + 1)
                V.tensor_copy(tb_[:, :, :], xw[:, :, 1, :])
                dve.drain()
                V.tensor_tensor(ta[:, :, :], yw[1], tb_[:, :, :], ALU.add)
                dve.drain()
                V.tensor_tensor(tb_[:, :, :], ta[:, :, :], over_rows(inv_deg[:, at]), ALU.mult)
                dve.drain()
                V.tensor_tensor(ta[:, :, :], xw[:, :, 0, :], tb_[:, :, :], ALU.add)
                dve.drain().then_inc(y_used, 1)
                V.tensor_tensor(tb_[:, :, :], ta[:, :, :], vec_rows(2), ALU.add)
                dve.drain()
                V.tensor_scalar(ta[:, :, :], tb_[:, :, :], 0.0, None, ALU.max)
                dve.drain()
                V.tensor_tensor(tb_[:, :, :], ta[:, :, :], ta[:, :, :], ALU.mult)
                dve.drain()
                V.reduce_sum(stat[:, 0, :], tb_[:, :, :], AX.X)
                dve.drain()
                V.tensor_scalar(stat[:, 1, :], stat[:, 0, :], L2_EPS * L2_EPS, None, ALU.max)
                to_power(2 * NB + NB + 2 * (n - NB) + 1)
                V.tensor_tensor(tb_[:, :, :], ta[:, :, :], over_rows(stat[:, 2, :]), ALU.mult)
                dve.drain()
                V.tensor_tensor(ta[:, :, :], tb_[:, :, :], rows[:, at, :], ALU.add)
                dve.drain()
                norm(ta[:, :, :], rows[:, at, :], 2 * NB + NB + 2 * (n - NB) + 2)
                new_rows(i, 2)

            def finish_t1(i, n):
                at = bass.ds(i * TB, TB)
                dve.wait_ge(xw_ready, n + 1)
                s = l3_sum[:, at, :]
                V.tensor_tensor(s, xw[:, :, 0, :], rows[:, at, :], ALU.add)
                dve.drain()
                for src, op in ((vec_rows(3), ALU.add), (yw[1], ALU.add), (xw[:, :, 1, :], ALU.subtract),
                                (yw[2], ALU.subtract)):
                    V.tensor_tensor(s, s, src, op)
                    dve.drain()
                V.tensor_copy(ta[:, :, :], yw[0])
                dve.drain().then_inc(y_used, 1)
                split_rows(ta[:, :, :], xs[1][:, at, 0, :], xs[1][:, at, 1, :]).then_inc(rows_ready, 1)
                dve.drain()

            def finish_t2(i, n):
                at = bass.ds(i * TB, TB)
                s = l3_sum[:, at, :]
                V.scalar_tensor_tensor(out=ta[:, :, :], in0=yw[0], scalar=2.0, in1=rows[:, at, :],
                                       op0=ALU.mult, op1=ALU.subtract)
                V.scalar_tensor_tensor(out=s, in0=yw[1], scalar=2.0, in1=s, op0=ALU.mult, op1=ALU.add)
                dve.drain().then_inc(y_used, 1)
                split_rows(ta[:, :, :], xs[0][:, at, 0, :], xs[0][:, at, 1, :]).then_inc(rows_ready, 1)
                dve.drain()

            def finish_l3(i, n):
                at = bass.ds(i * TB, TB)
                V.scalar_tensor_tensor(out=ta[:, :, :], in0=yw[0], scalar=2.0, in1=l3_sum[:, at, :],
                                       op0=ALU.mult, op1=ALU.add)
                dve.drain().then_inc(y_used, 1)
                norm(ta[:, :, :], rows[:, at, :], 2 * NB + NB + 2 * NB + n - 4 * NB + 1)
                dve.drain().then_inc(out_ready, 1)

            FINISH = (finish_l1, finish_l2, finish_t1, finish_t2, finish_l3)

            def row(k, i, before):
                for j in range(NB):
                    split_lo(BLOCKS * (k + 1) + NB * i + j, j)
                    if before and before[0] in X_TIMES:
                        if j == 0:
                            copy_x_block(before[1])
                        if j == 2:
                            copy_x_turned(NB * (before[0] - X_TIMES[0]) + before[1])
                    if j == 4 and before:
                        kb, ib = before
                        dve.wait_ge(y_back, NB + NB * kb + ib + 1)
                        FINISH[kb](ib, NB * kb + ib)

            for k in range(5):
                row(k, 0, (k - 1, NB - 1) if k > 0 else None)
                with dve.Fori(1, NB) as i:
                    row(k, i, (k, i - 1))
            dve.wait_ge(y_back, 6 * NB)
            FINISH[4](NB - 1, 5 * NB - 1)


_INS = ["x", "adj", "L0_gnn_W_u", "L0_gnn_diag_u", "L0_gnn_par_u", "L0_gnn_W_i", "L0_gnn_diag_i", "L0_gnn_par_i",
        "L0_gnn_ln_gamma", "L0_gnn_ln_beta", "L2_gnn_W", "L2_gnn_b", "L3_gnn_weight", "L3_gnn_bias"]


def kernel(**inputs):
    import numpy as np
    import concourse.bacc as bacc
    from concourse.bass_utils import run_bass_kernel_spmd

    nc = bacc.Bacc("TRN2", target_bir_lowering=False, num_devices=1)
    arrays, args = {}, []
    for name in _INS:
        a = np.ascontiguousarray(inputs[name])
        arrays[f"in_{name}"] = a
        args.append(nc.dram_tensor(f"in_{name}", a.shape, mybir.dt.from_np(a.dtype), kind="ExternalInput").ap())
    out = nc.dram_tensor("out_0", arrays["in_x"].shape, F32, kind="ExternalOutput").ap()
    build(nc, *args, out)
    r = run_bass_kernel_spmd(nc, [arrays], core_ids=[0])
    return r.results[0]["out_0"]
```

```python
from contextlib import ExitStack

import concourse.bass as bass
from concourse import mybir

F32 = mybir.dt.float32
F32R = mybir.dt.float32r
ALU = mybir.AluOpType
ACT = mybir.ActivationFunctionType
AX = mybir.AxisListType

P = 128
LN_EPS = 1e-5
L2_EPS = 1e-12


def build(nc, x, adj, w_u, diag_u, par_u, w_i, diag_i, par_i, gamma, beta, l2_w, l2_b, l3_w, l3_b, out):
    N, F = x.shape
    BLK = 512
    NB = N // BLK
    TB = BLK // P
    NT = N // P
    UB = diag_u.shape[0] // BLK
    UT = UB * TB
    RING = 8
    SWEEPS = 6
    HEAD = (0, 3, 3, 2, 2, 0)
    HT = TB // 2
    NAT = 5
    BLOCKS = NB * NB
    assert NB % NAT == 0 and NB % 2 == 0

    at_dram = nc.dram_tensor("a_transposed", [NB, NB, P, TB * BLK], F32, kind="Internal").ap()
    a_blocks = adj.rearrange("(t p) j -> p t j", p=P)
    x_rows = x.rearrange("(t p) f -> p t f", p=P)
    out_rows = out.rearrange("(t p) f -> p t f", p=P)

    ctx = ExitStack()
    with ctx:
        def sb(name, shape, dt=F32):
            return ctx.enter_context(nc.sbuf_tensor(name, shape, dt))

        def pb(name):
            return ctx.enter_context(nc.psum_tensor(name, [P, BLK], F32))

        def sem(name):
            return ctx.enter_context(nc.semaphore(name))

        at_raw = sb("at_raw", [P, NB, TB, BLK])
        at_hi = sb("at_hi", [P, 2 * 2, HT, BLK], F32R)
        at_lo = sb("at_lo", [P, 2 * 2, HT, BLK], F32R)
        rows = sb("rows", [P, NT, F])
        part = sb("part", [P, N])
        l3_sum = at_raw[:, RING:NB].rearrange("p s t n -> p (s t n)")[:, 0:NT * F]\
            .rearrange("p (t f) -> p t f", t=NT)
        row_part = sb("row_part", [P, NT, NB])
        inv_deg = sb("inv_deg", [P, NT])
        u_split = sb("u_split", [P, TB, 2, F], F32R)
        y_turned = sb("y_turned", [P, BLK])
        x_turned = sb("x_turned", [F, BLK])
        ta, tb_ = (sb(f"temp{k}", [P, TB, F]) for k in range(2))
        stats = sb("stats", [P, TB, nc.vector.BN_STATS_DIM])
        mean_var = sb("mean_var", [P, TB, nc.vector.BN_AGGR_DIM])
        row_sum = sb("row_sum", [P, TB])
        power_in = sb("power_in", [P, TB])
        power_out = sb("power_out", [P, TB])
        ident = sb("ident", [P, P])
        ident2 = sb("ident2", [P, F])
        w0 = sb("w0", [F, 2, F])
        w2x = sb("w2x", [F, 2, F])
        w3x = sb("w3x", [F, 2, F])
        twice = sb("twice", [P, 4, F])
        diag_flat = sb("diag_flat", [NT, P])
        diag = sb("diag", [P, NT])
        par = sb("par", [P, 2, 2])
        par_prod = sb("par_prod", [P, 2])
        vec = sb("vec", [P, 4, F])
        minus_half = sb("minus_half", [P, TB])

        with nc.sbuf_tensor("nat", [P, NAT, TB, BLK], F32) as nat:
            pass
        xs = [sb(f"xs{k}", [P, NT, 2, F], F32R) for k in range(2)]

        ps_t = [pb(f"ps_turn{k}") for k in range(TB)]
        ps_u = pb("ps_u")
        ps_h = [pb(f"ps_h{k}") for k in range(2)]
        ps_back = pb("ps_back")
        back = ps_back[:, 0:TB * F].rearrange("p (t f) -> p t f", t=TB)
        ps_y = ps_u
        ps_z = ps_h
        yw = [ps_t[k][:, 0:TB * F].rearrange("p (t f) -> p t f", t=TB) for k in range(3)]
        ps_xt = ps_t[3]
        xa = back
        ps_xt_in = ps_h[0]
        xw_in = ps_h[1][:, 0:TB * F].rearrange("p (t f) -> p t f", t=TB)

        consts_loaded = sem("consts_loaded")
        x_loaded = sem("x_loaded")
        x_reloaded = sem("x_reloaded")
        ident_ready = sem("ident_ready")
        diag_turned = sem("diag_turned")
        xt_ready = sem("xt_ready")
        xt_copied = sem("xt_copied")
        xw_ready = sem("xw_ready")
        xw_used = sem("xw_used")
        nat_loaded = [sem(f"nat_loaded{k}") for k in range(NAT)]
        nat_summed = sem("nat_summed")
        u_added = sem("u_added")
        u_copied = sem("u_copied")
        u_back = sem("u_back")
        u_ready = sem("u_ready")
        turned = sem("turned")
        at_evacuated = sem("at_evacuated")
        at_stored = [sem(f"at_stored{k}") for k in range(NB)]
        hi_ready = sem("hi_ready")
        lo_ready = sem("lo_ready")
        multiplied = sem("multiplied")
        h_free = sem("h_free")
        hy_ready = sem("hy_ready")
        raw_loaded = [sem(f"raw_loaded{k}") for k in range(RING)]
        z_copied = sem("z_copied")
        y_copied = sem("y_copied")
        y_back = sem("y_back")
        y_used = sem("y_used")
        var_ready = sem("var_ready")
        pow_ready = sem("pow_ready")
        rows_ready = sem("rows_ready")
        out_ready = sem("out_ready")
        stored = sem("stored")

        block = ctx.enter_context(nc.Block())
        N_CONSTS = 22
        N_ROOTS = 6 * NB
        X_TIMES = (1, 2)

        def at(s, r):
            return r if s % 2 == 0 else NB - 1 - r

        blocks = []
        after = {}

        def then(*what):
            after.setdefault(len(blocks) - 1, []).append(what)

        for s in range(SWEEPS):
            ends, begins = s > 0, s < SWEEPS - 1
            if ends and s > 0:
                then("turn", s, 0)
            head = HEAD[s]
            if ends and begins:
                for r in range(1, head + 1):
                    blocks += [(s, r, q, True, False) for q in range(r)]
                    then("turn", s, r)
                for r in range(head + 1):
                    blocks += [(s, r, q, False, True) for q in range(r + 1)]
                    then("keep", s, r)
                for r in range(head + 1, NB):
                    blocks += [(s, r, q, True, True) for q in range(r - 1)]
                    if r - 1 > head:
                        blocks += [(s, r - 1, r - 1, False, True)]
                        then("keep", s, r - 1)
                    blocks += [(s, r, r - 1, True, True)]
                    then("turn", s, r)
                blocks += [(s, NB - 1, NB - 1, False, True)]
                then("keep", s, NB - 1)
            else:
                for r in range(0 if begins else 1, NB):
                    blocks += [(s, r, q, ends, begins) for q in range(r + begins)]
                    then("keep" if begins else "turn", s, r)

        def opens(b, what):
            return blocks[b][what] and not any(c[:2] == blocks[b][:2] and c[what] for c in blocks[:b])

        def closes(b, what):
            return blocks[b][what] and not any(c[:2] == blocks[b][:2] and c[what] for c in blocks[b + 1:])

        def done(b):
            return 4 + 2 * (BLOCKS + b + 1)

        @block.sync
        def _(sp):
            sp.dma_start(rows[:, :, :], x_rows).then_inc(x_loaded, 16)

            def load(j, i):
                n = NB * j + i
                if not (isinstance(j, int) and j == 0 and i < NAT):
                    sp.wait_ge(u_added, n - NAT + 1)
                    sp.wait_ge(nat_summed, n - NAT + 1)
                sp.dma_start(nat[:, i % NAT], a_blocks[:, i * TB:(i + 1) * TB, bass.ds(j * BLK, BLK)])\
                    .then_inc(nat_loaded[i % NAT], 16)

            for i in range(NB):
                load(0, i)
            with sp.Fori(1, NB) as j:
                for i in range(NB):
                    load(j, i)
            sp.wait_ge(u_added, BLOCKS)
            sp.dma_start(rows[:, :, :], x_rows).then_inc(x_reloaded, 16)
            for s in at_stored:
                sp.wait_ge(s, 16 * NB)
            for b, (s, r, q, _, _) in enumerate(blocks):
                sp.wait_ge(lo_ready, 2 * (BLOCKS + b - RING + 1 if b >= RING else BLOCKS - NB + b + 1))
                sp.dma_start(at_raw[:, b % RING].rearrange("p t n -> p (t n)"), at_dram[at(s, r), at(s, q)])\
                    .then_inc(raw_loaded[b % RING], 16)
            for r in range(NB):
                sp.wait_ge(out_ready, r + 1)
                i = at(SWEEPS - 1, r)
                sp.dma_start(out_rows[:, i * TB:(i + 1) * TB, :], rows[:, i * TB:(i + 1) * TB, :])\
                    .then_inc(stored, 16)
            sp.wait_ge(stored, 16 * NB)

        @block.gpsimd
        def _(pool):
            nc.gpsimd.memset(ident[:, :], 0.0).then_inc(ident_ready, 1)
            pool.wait_ge(ident_ready, 1)
            nc.gpsimd.affine_select(out=ident[:, :], in_=ident[:, :], compare_op=ALU.not_equal, fill=1.0,
                                    base=0, pattern=[[-1, P]], channel_multiplier=1).then_inc(ident_ready, 1)

            with pool.Fori(0, N_ROOTS) as n:
                pool.wait_ge(var_ready, n + 1)
                nc.gpsimd.tensor_tensor(power_out[:, :], power_in[:, :], minus_half[:, :], ALU.pow)\
                    .then_inc(pow_ready, 1)

        @block.scalar
        def _(act):
            def const(dst, src):
                act.dma_start(dst, src).then_inc(consts_loaded, 16)

            const(diag_flat[0:UT, :], diag_u.rearrange("(t p) -> t p", p=P))
            const(diag_flat[UT:NT, :], diag_i.rearrange("(t p) -> t p", p=P))
            const(par[:, 0, :], par_u.partition_broadcast(P))
            const(par[:, 1, :], par_i.partition_broadcast(P))
            const(w0[:, 0, :], w_u)
            const(w0[:, 1, :], w_i)
            for k, v in enumerate((gamma, beta, l2_b, l3_b)):
                const(vec[:, k, :], v.partition_broadcast(P))
            const(w2x[:, 0, :], l2_w[0:F, :])
            const(w2x[:, 1, :], l2_w[F:2 * F, :])
            const(w3x[:, 0, :], l3_w[0])
            const(w3x[:, 1, :], l3_w[2])
            for h in range(2):
                half = slice(h * F, (h + 1) * F)
                const(twice[half, 0, :], l2_w[F:2 * F, :])
                for k in range(1, 4):
                    const(twice[half, k, :], l3_w[k])

            def split_hi(m, raw, slot):
                for h in range(2):
                    act.wait_ge(multiplied, 2 * m + h + 1)
                    nc.scalar.activation(at_hi[:, 2 * slot + h], at_raw[:, raw, h * HT:(h + 1) * HT],
                                         ACT.Copy).then_inc(hi_ready, 1)

            def store(j, i):
                act.wait_ge(at_evacuated, TB * (NB * j + i + 1))
                act.dma_start(at_dram[i, bass.ds(j, 1)].rearrange("o p n -> p (o n)"),
                              at_raw[:, i].rearrange("p t n -> p (t n)")).then_inc(at_stored[i], 16)

            def column(j, first):
                for i in range(NB):
                    if not first:
                        act.wait_ge(at_evacuated, TB * (NB * (j - 1) + i + 1))
                        split_hi(NB * (j - 1) + i, i, i % 2)
                    if i > 0:
                        store(j, i - 1)
                    if not first:
                        act.wait_ge(lo_ready, 2 * (NB * (j - 1) + i + 1))
                        act.wait_ge(at_stored[i], 16 * j)
                    for t in range(TB):
                        act.wait_ge(turned, TB * (NB * j + i) + t + 1)
                        nc.scalar.activation(at_raw[:, i, t, :], ps_t[t][:, :], ACT.Copy)\
                            .then_inc(at_evacuated, 1)
                store(j, NB - 1)

            column(0, True)
            with act.Fori(1, NB) as j:
                column(j, False)
            for i in range(NB):
                act.wait_ge(at_evacuated, TB * (BLOCKS - NB + i + 1))
                split_hi(BLOCKS - NB + i, i, i % 2)

            def copies(b):
                for what, s, r in after.get(b, ()):
                    if what == "keep":
                        act.wait_ge(multiplied, done(b))
                        act.wait_ge(y_back, NB * s + r + 1)
                        i = at(s, r)
                        nc.scalar.activation(part[:, i * BLK:(i + 1) * BLK], ps_z[(NB * s + r) % 2][:, :], ACT.Copy)\
                            .then_inc(z_copied, 1)
                        continue
                    act.wait_ge(y_back, NB * s + r)
                    if s - 1 in X_TIMES:
                        act.wait_ge(xt_ready, NB * (s - X_TIMES[0]) + r + 1)
                        nc.scalar.activation(x_turned[:, :], ps_xt[0:F, :], ACT.Copy).then_inc(xt_copied, 1)
                    if r > 0:
                        act.wait_ge(multiplied, done(b))
                        nc.scalar.activation(y_turned[:, :], ps_y[:, :], ACT.Copy).then_inc(y_copied, 1)

            for b in range(len(blocks)):
                act.wait_ge(raw_loaded[b % RING], 16 * (b // RING + 1))
                split_hi(BLOCKS + b, b % RING, b % 2)
                if b > 0:
                    copies(b - 1)
            copies(len(blocks) - 1)

        @block.tensor
        def _(pe):
            pe.sem_inc(multiplied, 4)
            pe.wait_ge(ident_ready, 2)
            pe.wait_ge(consts_loaded, 16 * N_CONSTS)
            pe.matmul(ps_back[:, 0:NT], diag_flat[:, :], ident[0:NT, 0:NT], start=True, stop=True)\
                .then_inc(diag_turned, 1)
            pe.wait_ge(x_loaded, 16)

            def turn_x_in(i):
                if i > 0:
                    pe.wait_ge(xt_copied, i)
                for t in range(TB):
                    mm = pe.transpose(ps_xt_in[0:F, t * P:(t + 1) * P], rows[:, i * TB + t, :], ident[:, :])
                mm.then_inc(xt_ready, 1)

            def times_w(i):
                pe.wait_ge(xt_copied, i + 1)
                if i > 0:
                    pe.wait_ge(xw_used, i)
                for t in range(TB):
                    mm = pe.matmul(xw_in[:, t, :], x_turned[:, t * P:(t + 1) * P], w0[:, int(i >= UB), :],
                                   start=True, stop=True)
                mm.then_inc(xw_ready, 1)

            def multiply(m, slot, products):
                for t in range(TB):
                    if t % HT == 0:
                        pe.wait_ge(lo_ready, 2 * m + t // HT + 1)
                    for left, acc, start, stop in products:
                        for half in (at_hi, at_lo):
                            mm = pe.matmul(acc[:, :], left[:, t].rearrange("p h f -> p (h f)"),
                                           half[:, 2 * slot + t // HT, t % HT, :],
                                           start=start and t == 0 and half is at_hi,
                                           stop=stop and t == TB - 1 and half is at_lo)
                    if t % HT == HT - 1:
                        mm.then_inc(multiplied, 1)

            def h_part(j, i):
                m = NB * j + i
                pe.wait_ge(h_free, m + 1)
                multiply(m, i % 2, [(u_split, ps_h[i % 2], True, True)])

            def u_turn_back(j):
                pe.wait_ge(u_copied, j + 1)
                for t in range(TB):
                    mm = pe.matmul(back[:, t, :], y_turned[:, t * P:(t + 1) * P], ident2[:, :],
                                   start=True, stop=True)
                mm.then_inc(u_back, 1)

            def column(j, first):
                for i in range(NB):
                    n = NB * j + i
                    if first and i + 1 < NB:
                        turn_x_in(i + 1)
                    pe.wait_ge(nat_loaded[i % NAT], 32 * j + 16 * (i // NAT + 1))
                    for t in range(TB):
                        if not (first and i == 0):
                            pe.wait_ge(at_evacuated, TB * (n - 1) + t + 1)
                        for c in range(TB):
                            mm = pe.transpose(ps_t[t][:, c * P:(c + 1) * P],
                                              nat[:, i % NAT, c, t * P:(t + 1) * P], ident[:, :])
                        mm.then_inc(turned, 1)
                    if first:
                        if i + 1 < NB:
                            times_w(i + 1)
                        pe.wait_ge(xw_used, i + 1)
                    elif i == 0:
                        pe.wait_ge(u_copied, j)
                    for c in range(TB):
                        side = slice(c % 2 * F, (c % 2 + 1) * F)
                        mm = pe.matmul(ps_u[side, :], rows[:, i * TB + c, :], nat[:, i % NAT, c, :],
                                       start=i == 0 and c < 2, stop=i == NB - 1 and c >= TB - 2)
                    mm.then_inc(u_added, 1)
                    if not first:
                        if i == 0:
                            u_turn_back(j - 1)
                            pe.wait_ge(u_ready, j)
                        else:
                            h_part(j - 1, i - 1)
                if not first:
                    h_part(j - 1, NB - 1)

            turn_x_in(0)
            times_w(0)
            column(0, True)
            with pe.Fori(1, NB) as j:
                column(j, False)
            u_turn_back(NB - 1)
            pe.wait_ge(u_ready, NB)

            for i in range(NB):
                h_part(NB - 1, i)
                pe.wait_ge(hy_ready, i + 1)
                if i > 0:
                    pe.wait_ge(y_used, i)
                for t in range(TB):
                    mm = pe.matmul(back[:, t, :], y_turned[:, t * P:(t + 1) * P], ident2[:, :],
                                   start=True, stop=True)
                mm.then_inc(y_back, 1)

            y_w = lambda k: twice[:, k, :]
            TURN = (((yw[0], ident2[:, :], None),),
                    ((yw[0], y_w(0), w2x[:, 1, :]), (xa, None, w2x[:, 0, :])),
                    ((yw[0], ident2[:, :], None), (yw[1], y_w(1), w3x[:, 0, :]), (yw[2], y_w(3), w3x[:, 1, :])),
                    ((yw[0], ident2[:, :], None), (yw[1], y_w(2), None)),
                    ((yw[0], y_w(3), None),))

            def turn_x(s, r):
                i = at(s, r)
                pe.wait_ge(rows_ready, NB * s - r)
                pe.wait_ge(y_used, NB * s + r)
                for t in range(TB):
                    mm = pe.transpose(ps_xt[0:F, t * P:(t + 1) * P], rows[:, i * TB + t, :], ident[:, :])
                mm.then_inc(xt_ready, 1)

            def turn(s, r):
                i = at(s, r)
                pe.wait_ge(z_copied, NB * s - r)
                if s - 1 in X_TIMES:
                    pe.wait_ge(xt_copied, NB * (s - X_TIMES[0]) + r + 1)
                if r > 0:
                    pe.wait_ge(y_copied, (NB - 1) * (s - 1) + r)
                pe.wait_ge(y_used, NB * s + r)
                for dst, w_product, w_x in TURN[s - 1]:
                    for t in range(TB):
                        cols = slice(t * P, (t + 1) * P)
                        terms = []
                        if w_product is not None:
                            terms.append((part[:, i * BLK + t * P:i * BLK + (t + 1) * P], w_product))
                            if r > 0:
                                terms.append((y_turned[:, cols], w_product))
                        if w_x is not None:
                            terms.append((x_turned[:, cols], w_x))
                        for n, (left, right) in enumerate(terms):
                            mm = pe.matmul(dst[:, t, :], left, right, start=n == 0, stop=n == len(terms) - 1)
                mm.then_inc(y_back, 1)

            for b, (s, r, q, ends, begins) in enumerate(blocks):
                for what, s_, r_ in after.get(b, ()):
                    if what == "turn" and s_ - 1 in X_TIMES:
                        turn_x(s_, r_)
                products = []
                j = at(s, q) * TB
                if ends:
                    pe.wait_ge(rows_ready, NB * s - q)
                    if opens(b, 3) and (NB - 1) * (s - 1) + r > 1:
                        pe.wait_ge(y_copied, (NB - 1) * (s - 1) + r - 1)
                    products.append((xs[(s - 1) % 2][:, j:j + TB], ps_y, opens(b, 3), closes(b, 3)))
                if begins:
                    pe.wait_ge(rows_ready, NB * s + q + 1)
                    if opens(b, 4) and NB * s + r > 1:
                        pe.wait_ge(z_copied, NB * s + r - 1)
                    products.append((xs[s % 2][:, j:j + TB], ps_z[(NB * s + r) % 2], opens(b, 4), closes(b, 4)))
                multiply(BLOCKS + b, b % 2, products)
                for what, s_, r_ in after.get(b, ()):
                    if what == "turn":
                        turn(s_, r_)

        @block.vector
        def _(dve):
            V = nc.vector

            def split_rows(src, dst_hi, dst_lo):
                V.tensor_copy(dst_hi, src)
                dve.drain()
                return V.tensor_tensor(dst_lo, src, dst_hi.bitcast(F32), ALU.subtract)

            V.memset(minus_half[:, :], -0.5)
            V.memset(part[:, 0:N // 2], 0.0).then_inc(h_free, 1)
            V.memset(part[:, N // 2:N], 0.0).then_inc(h_free, 1)
            dve.wait_ge(consts_loaded, 16 * N_CONSTS)
            dve.wait_ge(ident_ready, 2)
            V.tensor_tensor(ident2[:, :], ident[:, 0:F], ident[:, F:P], ALU.add)
            V.tensor_tensor(par_prod[:, :], par[:, :, 0], par[:, :, 1], ALU.mult)
            dve.drain()
            dve.wait_ge(diag_turned, 1)
            V.tensor_scalar(diag[:, 0:UT], ps_back[:, 0:UT], par_prod[:, 0:1], None, ALU.mult)
            V.tensor_scalar(diag[:, UT:NT], ps_back[:, UT:NT], par_prod[:, 1:2], None, ALU.mult)
            dve.drain()

            def make_e(i):
                tiles = slice(i * TB, (i + 1) * TB)
                dve.wait_ge(xt_ready, i + 1)
                V.tensor_copy(x_turned[:, :], ps_xt_in[0:F, :]).then_inc(xt_copied, 1)
                dve.wait_ge(xw_ready, i + 1)
                V.tensor_tensor(ta[:, :, :], xw_in,
                                diag[:, tiles].unsqueeze(2).broadcast_to([P, TB, F]), ALU.mult)
                dve.drain()
                V.tensor_tensor(rows[:, tiles, :], rows[:, tiles, :], ta[:, :, :], ALU.add).then_inc(xw_used, 1)
                dve.drain()

            def split_lo_half(m, raw, slot, h):
                dve.wait_ge(hi_ready, 2 * m + h + 1)
                V.tensor_tensor(at_lo[:, 2 * slot + h], at_raw[:, raw, h * HT:(h + 1) * HT],
                                at_hi[:, 2 * slot + h].bitcast(F32), ALU.subtract).then_inc(lo_ready, 1)

            def split_lo(m, raw):
                for h in range(2):
                    split_lo_half(m, raw, raw % 2, h)

            def add_h(j, i):
                m = NB * j + i
                dve.wait_ge(multiplied, 2 * m + 6)
                cols = slice(i * BLK, (i + 1) * BLK)
                V.tensor_tensor(part[:, cols], part[:, cols], ps_h[i % 2][:, :], ALU.add).then_inc(h_free, 1)

            def copy_u(j):
                dve.wait_ge(u_added, NB * j + NB)
                V.tensor_copy(y_turned[:, :], ps_u[:, :]).then_inc(u_copied, 1)

            def split_u(j):
                dve.wait_ge(u_back, j + 1)
                split_rows(back, u_split[:, :, 0, :], u_split[:, :, 1, :]).then_inc(u_ready, 1)

            def column(j, first):
                for i in range(NB):
                    if first and i + 1 < NB:
                        make_e(i + 1)
                    if not first:
                        if i == 0:
                            copy_u(j - 1)
                        split_lo(NB * (j - 1) + i, i)
                        if i == 0:
                            split_u(j - 1)
                        else:
                            add_h(j - 1, i - 1)
                    dve.wait_ge(nat_loaded[i % NAT], 32 * j + 16 * (i // NAT + 1))
                    V.reduce_sum(row_part[:, i * TB:(i + 1) * TB, bass.ds(j, 1)].rearrange("p t o -> p (t o)"),
                                 nat[:, i % NAT], AX.X).then_inc(nat_summed, 1)
                if not first:
                    add_h(j - 1, NB - 1)

            make_e(0)
            column(0, True)
            with dve.Fori(1, NB) as j:
                column(j, False)
            copy_u(NB - 1)
            split_lo(BLOCKS - NB, 0)
            split_u(NB - 1)
            dve.drain()
            V.reduce_sum(inv_deg[:, :], row_part[:, :, :], AX.X)
            dve.drain()
            V.tensor_scalar(inv_deg[:, :], inv_deg[:, :], 1.0, 1.0, ALU.add, ALU.max)
            dve.drain()
            V.reciprocal(inv_deg[:, :], inv_deg[:, :])

            roots = [0]

            def ask_power():
                dve.drain().then_inc(var_ready, 1)
                roots[0] += 1
                return roots[0]

            def over_rows(v):
                return v.unsqueeze(2).broadcast_to([P, TB, F])

            def vec_rows(k):
                return vec[:, k, :].unsqueeze(1).broadcast_to([P, TB, F])

            def rows_of(t, i):
                return t[:, i * TB:(i + 1) * TB]

            def norm(src, dst):
                for t in range(TB):
                    V.bn_stats(stats[:, t, :], src[:, t, :])
                dve.drain()
                for t in range(TB):
                    V.bn_aggr(mean_var[:, t, :], stats[:, t, :])
                dve.drain()
                V.tensor_scalar(power_in[:, :], mean_var[:, :, 1], LN_EPS, None, ALU.add)
                n = ask_power()
                yield
                dve.wait_ge(pow_ready, n)
                for t in range(TB):
                    V.tensor_scalar(dst[:, t, :], src[:, t, :], mean_var[:, t, 0:1], power_out[:, t:t + 1],
                                    ALU.subtract, ALU.mult)
                dve.drain()

            def split_vectors(src, k, i):
                hi, lo = rows_of(xs[k % 2], i)[:, :, 0, :], rows_of(xs[k % 2], i)[:, :, 1, :]
                split_rows(src, hi, lo).then_inc(rows_ready, 1)

            def end_l0(i):
                x_i = rows_of(rows, i)
                dve.wait_ge(y_back, i + 1)
                yield from norm(back, ta)
                dve.drain().then_inc(y_used, 1)
                V.tensor_tensor(tb_[:, :, :], ta[:, :, :], vec_rows(0), ALU.mult)
                dve.drain()
                V.tensor_tensor(ta[:, :, :], tb_[:, :, :], vec_rows(1), ALU.add)
                dve.drain()
                V.scalar_tensor_tensor(out=tb_[:, :, :], in0=x_i, scalar=2.0, in1=ta[:, :, :],
                                       op0=ALU.mult, op1=ALU.add)
                dve.drain()
                yield from norm(tb_, x_i)
                split_vectors(x_i, 0, i)

            def end_l1(i, n):
                x_i = rows_of(rows, i)
                dve.wait_ge(y_back, n + 1)
                V.tensor_tensor(ta[:, :, :], yw[0], x_i, ALU.mult)
                V.tensor_scalar(tb_[:, :, :], x_i, 0.9, 1.0, ALU.mult, ALU.add)
                dve.drain().then_inc(y_used, 1)
                V.reduce_sum(row_sum[:, :], ta[:, :, :], AX.X)
                dve.drain()
                V.tensor_scalar(row_sum[:, :], row_sum[:, :], 0.01, None, ALU.mult)
                dve.drain()
                yield
                V.tensor_tensor(ta[:, :, :], tb_[:, :, :], over_rows(row_sum[:, :]), ALU.subtract)
                dve.drain()
                yield from norm(ta, x_i)
                split_vectors(x_i, 1, i)

            def end_l2(i, n):
                x_i = rows_of(rows, i)
                dve.wait_ge(y_back, n + 1)
                V.tensor_tensor(ta[:, :, :], yw[0], over_rows(rows_of(inv_deg, i)), ALU.mult)
                dve.drain()
                V.tensor_tensor(tb_[:, :, :], xa, ta[:, :, :], ALU.add)
                dve.drain().then_inc(y_used, 1)
                yield
                V.tensor_tensor(ta[:, :, :], tb_[:, :, :], vec_rows(2), ALU.add)
                dve.drain()
                V.tensor_scalar(tb_[:, :, :], ta[:, :, :], 0.0, None, ALU.max)
                dve.drain()
                yield
                V.tensor_tensor(ta[:, :, :], tb_[:, :, :], tb_[:, :, :], ALU.mult)
                dve.drain()
                V.reduce_sum(row_sum[:, :], ta[:, :, :], AX.X)
                dve.drain()
                V.tensor_scalar(power_in[:, :], row_sum[:, :], L2_EPS * L2_EPS, None, ALU.max)
                root = ask_power()
                yield
                dve.wait_ge(pow_ready, root)
                V.tensor_tensor(ta[:, :, :], tb_[:, :, :], over_rows(power_out[:, :]), ALU.mult)
                dve.drain()
                V.tensor_tensor(tb_[:, :, :], ta[:, :, :], x_i, ALU.add)
                dve.drain()
                yield
                yield from norm(tb_, x_i)
                split_vectors(x_i, 2, i)

            def end_t1(i, n):
                dve.wait_ge(y_back, n + 1)
                split_vectors(yw[0], 3, i)
                total = rows_of(l3_sum, i)
                V.tensor_tensor(total, yw[1], rows_of(rows, i), ALU.add)
                dve.drain()
                yield
                V.tensor_tensor(total, total, yw[2], ALU.subtract)
                dve.drain().then_inc(y_used, 1)
                V.tensor_tensor(total, total, vec_rows(3), ALU.add)
                dve.drain()

            def end_t2(i, n):
                total = rows_of(l3_sum, i)
                dve.wait_ge(y_back, n + 1)
                V.scalar_tensor_tensor(out=ta[:, :, :], in0=yw[0], scalar=2.0, in1=rows_of(rows, i),
                                       op0=ALU.mult, op1=ALU.subtract)
                dve.drain()
                split_vectors(ta[:, :, :], 4, i)
                yield
                V.scalar_tensor_tensor(out=total, in0=yw[1], scalar=2.0, in1=total, op0=ALU.mult, op1=ALU.add)
                dve.drain().then_inc(y_used, 1)

            def end_l3(i, n):
                dve.wait_ge(y_back, n + 1)
                V.scalar_tensor_tensor(out=ta[:, :, :], in0=yw[0], scalar=2.0, in1=rows_of(l3_sum, i),
                                       op0=ALU.mult, op1=ALU.add)
                dve.drain().then_inc(y_used, 1)
                yield
                yield from norm(ta, rows_of(rows, i))
                dve.drain().then_inc(out_ready, 1)

            ENDS = (end_l1, end_l2, end_t1, end_t2, end_l3)

            dve.wait_ge(x_reloaded, 16)
            for i in range(NB):
                dve.wait_ge(multiplied, 2 * (BLOCKS - NB + i) + 6)
                if i > 0:
                    dve.wait_ge(y_back, i)
                V.tensor_tensor(y_turned[:, :], part[:, i * BLK:(i + 1) * BLK], ps_h[i % 2][:, :], ALU.add)
                dve.drain().then_inc(hy_ready, 1)
                dve.drain().then_inc(h_free, 1)
                if i + 1 < NB:
                    split_lo(BLOCKS - NB + i + 1, i + 1)
                for _ in end_l0(i):
                    pass

            def last_before(t, s, r):
                needs = [b for b in range(t + 1, len(blocks)) if blocks[b][0] == s and blocks[b][2] == r
                         and blocks[b][4]]
                turns = [b for b in range(t + 1, len(blocks)) if any(a[0] == "turn" for a in after.get(b, ()))]
                return min(needs[:1] + turns[:1] + [len(blocks)]) - 1

            waiting, OVER = [], object()
            for b in range(len(blocks)):
                while any(b > last + 2 for last, _ in waiting):
                    for _ in waiting.pop(0)[1]:
                        pass
                for h in range(2):
                    split_lo_half(BLOCKS + b, b % RING, b % 2, h)
                    if waiting and next(waiting[0][1], OVER) is OVER:
                        waiting.pop(0)
                for what, s, r in after.get(b - 1, ()):
                    if what == "turn":
                        waiting.append((last_before(b - 1, s, r), ENDS[s - 1](at(s, r), NB * s + r)))
            for what, s, r in after.get(len(blocks) - 1, ()):
                if what == "turn":
                    waiting.append((0, ENDS[s - 1](at(s, r), NB * s + r)))
            for _, end in waiting:
                for _ in end:
                    pass


_INS = ["x", "adj", "L0_gnn_W_u", "L0_gnn_diag_u", "L0_gnn_par_u", "L0_gnn_W_i", "L0_gnn_diag_i", "L0_gnn_par_i",
        "L0_gnn_ln_gamma", "L0_gnn_ln_beta", "L2_gnn_W", "L2_gnn_b", "L3_gnn_weight", "L3_gnn_bias"]


def kernel(**inputs):
    import numpy as np
    import concourse.bacc as bacc
    from concourse.bass_utils import run_bass_kernel_spmd

    nc = bacc.Bacc("TRN2", target_bir_lowering=False, num_devices=1)
    arrays, args = {}, []
    for name in _INS:
        a = np.ascontiguousarray(inputs[name])
        arrays[f"in_{name}"] = a
        args.append(nc.dram_tensor(f"in_{name}", a.shape, mybir.dt.from_np(a.dtype), kind="ExternalInput").ap())
    out = nc.dram_tensor("out_0", arrays["in_x"].shape, F32, kind="ExternalOutput").ap()
    build(nc, *args, out)
    r = run_bass_kernel_spmd(nc, [arrays], core_ids=[0])
    return r.results[0]["out_0"]
```

```python
from contextlib import ExitStack

import concourse.bass as bass
from concourse import mybir

F32 = mybir.dt.float32
F32R = mybir.dt.float32r
ALU = mybir.AluOpType
ACT = mybir.ActivationFunctionType
AX = mybir.AxisListType

P = 128
LN_EPS = 1e-5
L2_EPS = 1e-12


def build(nc, x, adj, w_u, diag_u, par_u, w_i, diag_i, par_i, gamma, beta, l2_w, l2_b, l3_w, l3_b, out):
    N, F = x.shape
    BLK = 512
    NB = N // BLK
    TB = BLK // P
    NT = N // P
    UB = diag_u.shape[0] // BLK
    UT = UB * TB
    MORE = 6
    SWEEPS = 6
    HEAD = (0,) + (SWEEPS - 1) * (2,)
    SLOW_ENDS = (1, 2)
    QUICK_ENDS = (3, 4)
    REACH = 12
    HOLD, HELD = (3, 5), 3
    HT = TB // 2
    NAT = 5
    BLOCKS = NB * NB
    assert NB % NAT == 0 and NB % 2 == 0

    at_dram = nc.dram_tensor("a_transposed", [NB, NB, P, TB * BLK], F32, kind="Internal").ap()
    a_blocks = adj.rearrange("(t p) j -> p t j", p=P)
    x_rows = x.rearrange("(t p) f -> p t f", p=P)
    out_rows = out.rearrange("(t p) f -> p t f", p=P)

    ctx = ExitStack()
    with ctx:
        def sb(name, shape, dt=F32):
            return ctx.enter_context(nc.sbuf_tensor(name, shape, dt))

        def pb(name):
            return ctx.enter_context(nc.psum_tensor(name, [P, BLK], F32))

        def sem(name):
            return ctx.enter_context(nc.semaphore(name))

        at_raw = sb("at_raw", [P, NB, TB, BLK])
        rows = sb("rows", [P, NT, F])
        part = sb("part", [P, N])
        row_part = sb("row_part", [P, NT, NB])
        inv_deg = sb("inv_deg", [P, NT])
        u_split = sb("u_split", [P, TB, 2, F], F32R)
        u_turned = sb("u_turned", [P, BLK])
        x_turned = u_turned[0:F, :]
        ta, tb_, tc, centred = (sb(f"temp{k}", [P, TB, F]) for k in range(4))
        stats = sb("stats", [P, TB, nc.vector.BN_STATS_DIM])
        mean_var = sb("mean_var", [P, TB, nc.vector.BN_AGGR_DIM])
        row_sum = sb("row_sum", [P, TB])
        power_in = sb("power_in", [P, TB])
        power_out = sb("power_out", [P, TB])
        ident = sb("ident", [P, P])
        ident2 = sb("ident2", [P, F])
        w0 = sb("w0", [F, 2, F])
        w2x = sb("w2x", [F, 2, F])
        w3x = sb("w3x", [F, 2, F])
        twice = sb("twice", [P, 4, F])
        diag_flat = sb("diag_flat", [NT, P])
        diag = sb("diag", [P, NT])
        par = sb("par", [P, 2, 2])
        par_prod = sb("par_prod", [P, 2])
        vec = sb("vec", [P, 4, F])
        minus_half = sb("minus_half", [P, TB])

        with nc.sbuf_tensor("at_hi", [P, 2 * 2, HT, BLK], F32R) as at_hi, \
                nc.sbuf_tensor("at_lo", [P, 2 * 2, HT, BLK], F32R) as at_lo, \
                nc.sbuf_tensor("nat", [P, NAT, TB, BLK], F32) as nat, \
                nc.sbuf_tensor("e", [P, NT, F], F32) as e_rows:
            pass
        OVER_HALVES = 4
        at_more = sb("at_more", [P, MORE, TB, BLK])
        vectors = sb("vectors", [P, NT, 2, F])
        base = sb("base", [P, NT, F])

        u_last = tc

        ps_t = [pb(f"ps_turn{k}") for k in range(TB)]
        ps_u = pb("ps_u")
        ps_h = [pb(f"ps_h{k}") for k in range(2)]
        ps_back = pb("ps_back")
        back = ps_back[:, 0:TB * F].rearrange("p (t f) -> p t f", t=TB)
        ps_both = [ps_u, ps_back]
        ps_own = [ps_h, [ps_u, ps_t[2]]]
        yw = [[ps_t[n][:, k * TB * F:(k + 1) * TB * F].rearrange("p (t f) -> p t f", t=TB) for k in range(2)]
              for n in range(2)]
        ps_xt = ps_t[3]
        xw = ps_t[2][:, :].rearrange("p (t f) -> p t f", t=TB)
        ps_xt_in = ps_h[0]
        xw_in = ps_h[1][:, 0:TB * F].rearrange("p (t f) -> p t f", t=TB)

        consts_loaded = sem("consts_loaded")
        weights_loaded = sem("weights_loaded")
        x_first_loaded = sem("x_first_loaded")
        x_loaded = sem("x_loaded")
        ident_ready = sem("ident_ready")
        diag_turned = sem("diag_turned")
        xt_ready = sem("xt_ready")
        xt_copied = sem("xt_copied")
        xw_ready = sem("xw_ready")
        xw_used = sem("xw_used")
        nat_loaded = [sem(f"nat_loaded{k}") for k in range(NAT)]
        nat_summed = sem("nat_summed")
        u_added = sem("u_added")
        u_copied = sem("u_copied")
        u_back = sem("u_back")
        u_ready = sem("u_ready")
        turned = sem("turned")
        at_evacuated = sem("at_evacuated")
        at_stored = [sem(f"at_stored{k}") for k in range(NB)]
        hi_ready = sem("hi_ready")
        lo_ready = sem("lo_ready")
        multiplied = sem("multiplied")
        h_free = sem("h_free")
        last_h_done = sem("last_h_done")
        hy_ready = sem("hy_ready")
        raw_loaded = [sem(f"raw_loaded{k}") for k in range(NB + MORE)]
        block_done = sem("block_done")
        own_copied = sem("own_copied")
        kept = sem("kept")
        y_added = sem("y_added")
        y_back = sem("y_back")
        y_used = sem("y_used")
        var_ready = sem("var_ready")
        pow_ready = sem("pow_ready")
        rows_ready = sem("rows_ready")
        out_ready = sem("out_ready")
        stored = sem("stored")

        block = ctx.enter_context(nc.Block())
        N_CONSTS, N_WEIGHTS = 6, 16
        N_ROOTS = 6 * NB
        BASES = (1, 2)

        def at(s, r):
            return NB - 1 - r if s % 2 == 0 else r

        BOTH, END, BEGIN = range(3)
        blocks = []
        after, mid, ahead = {}, {}, {}

        def then(what, s, r, where=None):
            after.setdefault(len(blocks), []).append((what, s, r))
            if where is not None:
                where.setdefault(len(blocks), []).append((what, s, r))

        for s in range(SWEEPS):
            head = HEAD[s]
            if s == SWEEPS - 1:
                for r in range(head + 1, NB):
                    blocks += [(s, r, q, END) for q in range(r)]
                    then("turn", s, r, mid)
                break
            if s == 0:
                for r in range(NB - 1):
                    blocks += [(s, r, q, BEGIN) for q in range(r + 1)]
                    then("keep", s, r)
                blocks += [(s, NB - 1, q, BEGIN) for q in range(NB - 1)]
            else:
                for c in range(head + 1):
                    for r in range(c, head + 1):
                        blocks += [(s, r, c, BEGIN)]
                        if r == c:
                            then("keep", s, r)
                    if c > 0:
                        blocks += [(s, head + 1, c - 1, BOTH)]
                blocks += [(s, head + 1, head, BOTH)]
                then("turn", s, head + 1, mid)
                for r in range(head + 2, NB - 1):
                    blocks += [(s, r, q, BOTH) for q in range(r - 1)] + [(s, r - 1, r - 1, BEGIN)]
                    then("keep", s, r - 1)
                    blocks += [(s, r, r - 1, BOTH)]
                    then("turn", s, r, mid)
                r = NB - 1
                blocks += [(s, r, q, BOTH) for q in range(r - 1)]
                for q in (r - 1, r) if s in SLOW_ENDS else (r, r - 1):
                    if q == r:
                        blocks += [(s, r - 1, r - 1, BEGIN)]
                        then("keep", s, r - 1)
                    else:
                        blocks += [(s, r, q, BOTH)]
                        then("turn", s, r, mid)
            after_head = HEAD[s + 1]
            blocks += [(s + 1, r, q, END) for r in range(after_head, 1, -1) for q in range(1, r)]
            blocks += [(s, NB - 1, NB - 1, BEGIN)]
            then("keep", s, NB - 1)
            then("turn", s + 1, 0, mid)
            blocks += [(s + 1, r, 0, END) for r in range(after_head, 0, -1)]
            for r in range(1, after_head + 1):
                then("turn", s + 1, r, ahead if s + 1 < SWEEPS - 1 else mid)

        turn_at = {(s, r): b for b, events in after.items() for what, s, r in events if what == "turn"}
        for s in BASES:
            for r in range(NB):
                if r < 4:
                    b = turn_at[s, 4] + 1 + r
                elif r < NB - 2:
                    b = turn_at[s, r + 1] + 3
                elif r == NB - 2:
                    b = turn_at[s, NB - 1]
                else:
                    b = turn_at[s + 1, 0] - 1
                mid.setdefault(b, []).append(("turn_x", s, r))
                mid.setdefault(b + 1, []).insert(0, ("times_x", s, r))
                after.setdefault(b, []).append(("copy_x", s, r))
                events = after.setdefault(b + 1, [])
                if ("turn", s + 1, 0) in events:
                    events.insert(events.index(("turn", s + 1, 0)), ("base", s, r))
                else:
                    events.append(("base", s, r))

        group = [("own" if which == BEGIN else "both", s, r) for s, r, q, which in blocks]

        def opens(b):
            return group[b] not in group[:b]

        def closes(b):
            return group[b] not in group[b + 1:]

        in_both = [(s, r) for s in range(1, SWEEPS - 1) for r in range(HEAD[s] + 1, NB)]

        def n_kept(s, r):
            return sum(k <= (s, r) for k in in_both)

        spans, span_of = [[(i, NB - 1), []] for i in range(NB)], []
        for b, (s, r, q, which) in enumerate(blocks):
            key = at(s, r), at(s, q)
            found = [n for n in range(len(spans)) if spans[n][0] == key
                     and (n < NB and not spans[n][1]
                          or spans[n][1] and (b - spans[n][1][-1] <= REACH or s in HOLD and q < r <= HELD))]
            if found:
                spans[found[-1]][1].append(b)
                span_of.append(found[-1])
            else:
                span_of.append(len(spans))
                spans.append([key, [b]])
        last_use = [spans[i][1][-1] for i in range(NB)] + [-1] * OVER_HALVES \
            + [-2] * (MORE - OVER_HALVES)
        uses = [1 if n < NB else 0 for n in range(NB + MORE)]
        slot_of = list(range(NB))
        loads = []
        load_no = [0] * NB
        for key, its in spans[NB:]:
            slot = min(range(NB + MORE), key=lambda n: last_use[n])
            assert last_use[slot] < its[0]
            slot_of.append(slot)
            loads.append((key, slot, last_use[slot], uses[slot] == 0))
            load_no.append(sum(1 for l in loads if l[1] == slot))
            last_use[slot] = its[-1]
            uses[slot] += 1

        def raw(slot):
            return at_raw[:, slot] if slot < NB else at_more[:, slot - NB]

        def half(k):
            return slice(k % 2 * F, (k % 2 + 1) * F)

        def y_parts(s, r):
            return slice(0, P) if s == SWEEPS - 1 or r <= HEAD[s] else half(s - 1)

        @block.sync
        def _(sp):
            sp.dma_start(rows[:, 0:TB, :], x_rows[:, 0:TB, :]).then_inc(x_first_loaded, 16)
            for dst, src in ((par[:, 0, :], par_u.partition_broadcast(P)),
                             (par[:, 1, :], par_i.partition_broadcast(P)), (w0[:, 1, :], w_i)):
                sp.dma_start(dst, src).then_inc(consts_loaded, 16)

            def load(j, i):
                n = NB * j + i
                if not (isinstance(j, int) and j == 0 and i < NAT):
                    sp.wait_ge(u_added, n - NAT + 1)
                    sp.wait_ge(nat_summed, n - NAT + 1)
                sp.dma_start(nat[:, i % NAT], a_blocks[:, i * TB:(i + 1) * TB, bass.ds(j * BLK, BLK)])\
                    .then_inc(nat_loaded[i % NAT], 16)

            for i in range(NB):
                load(0, i)
                if i == 0:
                    sp.dma_start(rows[:, TB:NT, :], x_rows[:, TB:NT, :]).then_inc(x_loaded, 16)
            with sp.Fori(1, NB) as j:
                for i in range(NB):
                    load(j, i)
            columns_there = [0] * NB
            for (i, j), slot, b, first in loads:
                if columns_there[i] <= j:
                    sp.wait_ge(at_stored[i], 16 * (j + 1))
                    columns_there[i] = j + 1
                if not first:
                    sp.wait_ge(block_done, b + 1)
                    if slot < NB and columns_there[slot] < NB:
                        sp.wait_ge(at_stored[slot], 16 * NB)
                        columns_there[slot] = NB
                elif slot < NB + OVER_HALVES:
                    sp.wait_ge(multiplied, 2 * (BLOCKS - NB) + 4)
                else:
                    n_last = BLOCKS - NAT + slot - NB - OVER_HALVES
                    sp.wait_ge(u_added, n_last + 1)
                    sp.wait_ge(nat_summed, n_last + 1)
                sp.dma_start(raw(slot).rearrange("p t n -> p (t n)"), at_dram[i, j])\
                    .then_inc(raw_loaded[slot], 16)
            for r in range(NB):
                sp.wait_ge(out_ready, r + 1)
                i = at(SWEEPS - 1, r)
                sp.dma_start(out_rows[:, i * TB:(i + 1) * TB, :], rows[:, i * TB:(i + 1) * TB, :])\
                    .then_inc(stored, 16)
            sp.wait_ge(stored, 16 * NB)

        @block.gpsimd
        def _(pool):
            nc.gpsimd.memset(ident[:, :], 0.0).then_inc(ident_ready, 1)
            pool.wait_ge(ident_ready, 1)
            nc.gpsimd.affine_select(out=ident[:, :], in_=ident[:, :], compare_op=ALU.not_equal, fill=1.0,
                                    base=0, pattern=[[-1, P]], channel_multiplier=1).then_inc(ident_ready, 1)

            with pool.Fori(0, N_ROOTS) as n:
                pool.wait_ge(var_ready, n + 1)
                nc.gpsimd.tensor_tensor(power_out[:, :], power_in[:, :], minus_half[:, :], ALU.pow)\
                    .then_inc(pow_ready, 1)

        @block.scalar
        def _(act):
            def const(dst, src, loaded=consts_loaded):
                act.dma_start(dst, src).then_inc(loaded, 16)

            const(diag_flat[0:UT, :], diag_u.rearrange("(t p) -> t p", p=P))
            const(diag_flat[UT:NT, :], diag_i.rearrange("(t p) -> t p", p=P))
            const(w0[:, 0, :], w_u)
            act.wait_ge(nat_loaded[0], 16)
            for k, v in enumerate((gamma, beta, l2_b, l3_b)):
                const(vec[:, k, :], v.partition_broadcast(P), weights_loaded)
            const(w2x[:, 0, :], l2_w[0:F, :], weights_loaded)
            const(w2x[:, 1, :], l2_w[F:2 * F, :], weights_loaded)
            const(w3x[:, 0, :], l3_w[0], weights_loaded)
            const(w3x[:, 1, :], l3_w[2], weights_loaded)
            for h in range(2):
                half = slice(h * F, (h + 1) * F)
                const(twice[half, 0, :], l2_w[F:2 * F, :], weights_loaded)
                for k in range(1, 4):
                    const(twice[half, k, :], l3_w[k], weights_loaded)

            def split_hi(m, raw, slot):
                for h in range(2):
                    act.wait_ge(multiplied, 2 * m + h + 1)
                    nc.scalar.activation(at_hi[:, 2 * slot + h], at_raw[:, raw, h * HT:(h + 1) * HT],
                                         ACT.Copy).then_inc(hi_ready, 1)

            def store(j, i):
                act.wait_ge(at_evacuated, TB * (NB * j + i + 1))
                act.dma_start(at_dram[i, bass.ds(j, 1)].rearrange("o p n -> p (o n)"),
                              at_raw[:, i].rearrange("p t n -> p (t n)")).then_inc(at_stored[i], 16)

            def column(j, first):
                for i in range(NB):
                    if not first:
                        act.wait_ge(at_evacuated, TB * (NB * (j - 1) + i + 1))
                        split_hi(NB * (j - 1) + i, i, i % 2)
                    if i > 0:
                        store(j, i - 1)
                    if not first:
                        act.wait_ge(lo_ready, 2 * (NB * (j - 1) + i + 1))
                        act.wait_ge(at_stored[i], 16 * j)
                    for t in range(TB):
                        act.wait_ge(turned, TB * (NB * j + i) + t + 1)
                        nc.scalar.activation(at_raw[:, i, t, :], ps_t[t][:, :], ACT.Copy)\
                            .then_inc(at_evacuated, 1)
                store(j, NB - 1)

            column(0, True)
            with act.Fori(1, NB) as j:
                column(j, False)

            def keep_own(b, s, r):
                act.wait_ge(block_done, b)
                act.wait_ge(y_back, NB * s + r + 1)
                i = at(s, r)
                nc.scalar.activation(part[:, i * BLK:(i + 1) * BLK], ps_own[s == 0][r % 2][:, :],
                                     ACT.Copy).then_inc(own_copied, 1)

            for b in sorted(after):
                for what, s, r in after[b]:
                    if what == "keep":
                        keep_own(b, s, r)
                    if what == "copy_x":
                        if (s, r) > (BASES[0], 0):
                            act.wait_ge(xw_ready, NB * s + r)
                        act.wait_ge(xt_ready, NB * s + r + 1)
                        nc.scalar.activation(x_turned, ps_xt[0:F, :], ACT.Copy).then_inc(xt_copied, 1)

        @block.tensor
        def _(pe):
            pe.sem_inc(multiplied, 4)
            pe.wait_ge(ident_ready, 2)
            pe.wait_ge(consts_loaded, 16 * N_CONSTS)
            pe.matmul(ps_back[:, 0:NT], diag_flat[:, :], ident[0:NT, 0:NT], start=True, stop=True)\
                .then_inc(diag_turned, 1)
            pe.wait_ge(x_first_loaded, 16)

            def turn_x_in(i):
                if i > 0:
                    pe.wait_ge(xt_copied, i)
                    pe.wait_ge(x_loaded, 16)
                for t in range(TB):
                    mm = pe.transpose(ps_xt_in[0:F, t * P:(t + 1) * P], rows[:, i * TB + t, :], ident[:, :])
                mm.then_inc(xt_ready, 1)

            def times_w(i):
                pe.wait_ge(xt_copied, i + 1)
                if i > 0:
                    pe.wait_ge(xw_used, i)
                for t in range(TB):
                    mm = pe.matmul(xw_in[:, t, :], x_turned[:, t * P:(t + 1) * P], w0[:, int(i >= UB), :],
                                   start=True, stop=True)
                mm.then_inc(xw_ready, 1)

            def multiply(m, slot, products):
                for t in range(TB):
                    if t % HT == 0:
                        pe.wait_ge(lo_ready, 2 * m + t // HT + 1)
                    for left, acc, start, stop in products:
                        for half in (at_hi, at_lo):
                            mm = pe.matmul(acc[:, :], left[:, t].rearrange("p h f -> p (h f)"),
                                           half[:, 2 * slot + t // HT, t % HT, :],
                                           start=start and t == 0 and half is at_hi,
                                           stop=stop and t == TB - 1 and half is at_lo)
                    if t % HT == HT - 1:
                        mm.then_inc(multiplied, 1)

            def h_part(j, i):
                m = NB * j + i
                pe.wait_ge(h_free, m + 1)
                multiply(m, i % 2, [(u_split, ps_h[i % 2], True, True)])

            def u_turn_back(j):
                pe.wait_ge(u_copied, j + 1)
                for t in range(TB):
                    mm = pe.matmul(back[:, t, :], u_turned[:, t * P:(t + 1) * P], ident2[:, :],
                                   start=True, stop=True)
                mm.then_inc(u_back, 1)

            def column(j, first):
                for i in range(NB):
                    n = NB * j + i
                    if first and i + 1 < NB:
                        turn_x_in(i + 1)
                    pe.wait_ge(nat_loaded[i % NAT], 32 * j + 16 * (i // NAT + 1))
                    for t in range(TB):
                        if not (first and i == 0):
                            pe.wait_ge(at_evacuated, TB * (n - 1) + t + 1)
                        for c in range(TB):
                            mm = pe.transpose(ps_t[t][:, c * P:(c + 1) * P],
                                              nat[:, i % NAT, c, t * P:(t + 1) * P], ident[:, :])
                        mm.then_inc(turned, 1)
                    if first:
                        if i + 1 < NB:
                            times_w(i + 1)
                        pe.wait_ge(xw_used, i + 1)
                    elif i == 0:
                        pe.wait_ge(u_copied, j)
                    for c in range(TB):
                        side = slice(c % 2 * F, (c % 2 + 1) * F)
                        mm = pe.matmul(ps_u[side, :], e_rows[:, i * TB + c, :], nat[:, i % NAT, c, :],
                                       start=i == 0 and c < 2, stop=i == NB - 1 and c >= TB - 2)
                    mm.then_inc(u_added, 1)
                    if not first:
                        if i == 0:
                            u_turn_back(j - 1)
                            pe.wait_ge(u_ready, j)
                        else:
                            h_part(j - 1, i - 1)
                if not first:
                    h_part(j - 1, NB - 1)

            turn_x_in(0)
            times_w(0)
            column(0, True)
            with pe.Fori(1, NB) as j:
                column(j, False)
            u_turn_back(NB - 1)
            pe.wait_ge(u_ready, NB)

            as_it_is = ident2[:, :]
            TURN = (None, (as_it_is,), (twice[:, 0, :],), (as_it_is, twice[:, 1, :]),
                    (as_it_is, twice[:, 2, :]), (twice[:, 3, :],))

            def turn(s, r):
                i, n = at(s, r), NB * s + r
                if r > 0:
                    pe.wait_ge(y_added, (NB - 1) * (s - 1) + r)
                else:
                    pe.wait_ge(own_copied, NB * s)
                    if n_kept(s - 1, NB - 1) > 0:
                        pe.wait_ge(kept, n_kept(s - 1, NB - 1))
                pe.wait_ge(y_used, n - 1)
                for k, weights in enumerate(TURN[s]):
                    for t in range(TB):
                        mm = pe.matmul(yw[n % 2][k][:, t, :], part[:, i * BLK + t * P:i * BLK + (t + 1) * P],
                                       weights, start=True, stop=True)
                mm.then_inc(y_back, 1)

            def turn_x(s, r):
                pe.wait_ge(rows_ready, NB * s + r + 1)
                if (s, r) > (BASES[0], 0):
                    pe.wait_ge(xt_copied, NB * s + r)
                for t in range(TB):
                    mm = pe.transpose(ps_xt[0:F, t * P:(t + 1) * P], vectors[:, at(s, r) * TB + t, s % 2, :],
                                      ident[:, :])
                mm.then_inc(xt_ready, 1)

            def times_x(s, r):
                pe.wait_ge(xt_copied, NB * s + r + 1)
                if (s, r) > (BASES[0], 0):
                    pe.wait_ge(xw_used, NB * s + r)
                else:
                    pe.wait_ge(own_copied, NB)
                weights = w2x[:, :, :].rearrange("p k f -> p (k f)") if s == 1 else w3x[:, 0, :]
                for t in range(TB):
                    mm = pe.matmul(xw[:, t, 0:(2 if s == 1 else 1) * F], x_turned[:, t * P:(t + 1) * P],
                                   weights, start=True, stop=True)
                mm.then_inc(xw_ready, 1)

            DO = {"turn": turn, "turn_x": turn_x, "times_x": times_x}

            def multiply_block(b):
                for what, s, r in ahead.get(b, ()):
                    DO[what](s, r)
                s, r, q, which = blocks[b]
                if load_no[span_of[b]] > 0:
                    pe.wait_ge(raw_loaded[slot_of[span_of[b]]], 16 * load_no[span_of[b]])
                if which != BEGIN:
                    pe.wait_ge(rows_ready, NB * s - q)
                if which != END:
                    pe.wait_ge(rows_ready, NB * s + q + 1)
                start, stop = opens(b), closes(b)
                if start and group[b][0] == "own":
                    if NB * s + r > 1:
                        pe.wait_ge(own_copied, NB * s + r - 1)
                elif start:
                    ps, pr = (s, r - 2) if r > 2 else (s - 1, NB - (2 if r == 2 else 1))
                    if ps > 0:
                        pe.wait_ge(y_added, (NB - 1) * (ps - 1) + pr)
                        if n_kept(ps, pr) > 0:
                            pe.wait_ge(kept, n_kept(ps, pr))
                    elif r == 2:
                        pe.wait_ge(own_copied, NB - 1)
                bank = ps_own[s == 0][r % 2] if which == BEGIN else ps_both[r % 2]
                tiles = raw(slot_of[span_of[b]])
                for t in range(TB):
                    if t == HT:
                        for what, s_then, r_then in mid.get(b, ()):
                            DO[what](s_then, r_then)
                    vs = vectors[:, at(s, q) * TB + t]
                    first, last = start and t == 0, stop and t == TB - 1
                    if which == BOTH:
                        left, acc = vs.rearrange("p h f -> p (h f)"), bank[:, :]
                    else:
                        k = s - 1 if which == END else s
                        left = vs[:, k % 2, :]
                        acc = bank[half(t), :]
                        first, last = start and t < 2, stop and t >= TB - 2
                    mm = pe.matmul(acc, left, tiles[:, t, :], start=first, stop=last)
                mm.then_inc(block_done, 1)

            def last_h_part(e):
                if e < 2:
                    pe.wait_ge(h_free, BLOCKS - NB + e + 1)
                else:
                    pe.wait_ge(hy_ready, e - 1)
                for t in range(TB):
                    mm = pe.matmul(ps_h[e % 2][half(t), :], u_last[:, t, :], at_raw[:, NB - 1 - e, t, :],
                                   start=t < 2, stop=t >= TB - 2)
                mm.then_inc(last_h_done, 1)

            row_0 = [[b for b in range(len(blocks)) if blocks[b][0] == 0 and blocks[b][1] == r]
                     for r in range(NB - 2)]
            pe.wait_ge(at_evacuated, TB * BLOCKS)
            last_h_part(0)
            for e in range(NB):
                i = NB - 1 - e
                pe.wait_ge(hy_ready, e + 1)
                if e > 1:
                    pe.wait_ge(y_used, e - 1)
                for t in range(TB):
                    mm = pe.matmul(yw[e % 2][0][:, t, :], part[:, i * BLK + t * P:i * BLK + (t + 1) * P], ident2[:, :],
                                   start=True, stop=True)
                mm.then_inc(y_back, 1)
                for k in range(1 if e == 0 else e + 2, min(e + 3, NB)):
                    last_h_part(k)
                for b in row_0[e - 1] if 1 <= e <= NB - 2 else ():
                    multiply_block(b)

            for b in range(len(row_0) * (len(row_0) + 1) // 2, len(blocks)):
                multiply_block(b)
            for what, s, r in mid.get(len(blocks), ()):
                DO[what](s, r)

        @block.vector
        def _(dve):
            V = nc.vector

            def split_rows(src, dst_hi, dst_lo):
                V.tensor_copy(dst_hi, src)
                dve.drain()
                return V.tensor_tensor(dst_lo, src, dst_hi.bitcast(F32), ALU.subtract)

            V.memset(minus_half[:, :], -0.5)
            V.memset(part[:, 0:N // 2], 0.0).then_inc(h_free, 1)
            V.memset(part[:, N // 2:N], 0.0).then_inc(h_free, 1)
            dve.wait_ge(ident_ready, 2)
            dve.wait_ge(consts_loaded, 16 * N_CONSTS)
            V.tensor_tensor(ident2[:, :], ident[:, 0:F], ident[:, F:P], ALU.add)
            V.tensor_tensor(par_prod[:, :], par[:, :, 0], par[:, :, 1], ALU.mult)
            dve.drain()
            dve.wait_ge(diag_turned, 1)
            V.tensor_scalar(diag[:, 0:UT], ps_back[:, 0:UT], par_prod[:, 0:1], None, ALU.mult)
            V.tensor_scalar(diag[:, UT:NT], ps_back[:, UT:NT], par_prod[:, 1:2], None, ALU.mult)
            dve.drain()

            def make_e(i):
                tiles = slice(i * TB, (i + 1) * TB)
                dve.wait_ge(xt_ready, i + 1)
                V.tensor_copy(x_turned, ps_xt_in[0:F, :]).then_inc(xt_copied, 1)
                dve.wait_ge(xw_ready, i + 1)
                V.tensor_tensor(ta[:, :, :], xw_in,
                                diag[:, tiles].unsqueeze(2).broadcast_to([P, TB, F]), ALU.mult)
                dve.drain()
                V.tensor_tensor(e_rows[:, tiles, :], rows[:, tiles, :], ta[:, :, :], ALU.add).then_inc(xw_used, 1)
                dve.drain()

            def split_lo_half(m, raw, slot, h):
                dve.wait_ge(hi_ready, 2 * m + h + 1)
                V.tensor_tensor(at_lo[:, 2 * slot + h], at_raw[:, raw, h * HT:(h + 1) * HT],
                                at_hi[:, 2 * slot + h].bitcast(F32), ALU.subtract).then_inc(lo_ready, 1)

            def split_lo(m, raw, slot):
                for h in range(2):
                    split_lo_half(m, raw, slot, h)

            def add_h(j, i):
                m = NB * j + i
                dve.wait_ge(multiplied, 2 * m + 6)
                cols = slice(i * BLK, (i + 1) * BLK)
                V.tensor_tensor(part[:, cols], part[:, cols], ps_h[i % 2][:, :], ALU.add).then_inc(h_free, 1)

            def copy_u(j):
                dve.wait_ge(u_added, NB * j + NB)
                V.tensor_copy(u_turned[:, :], ps_u[:, :]).then_inc(u_copied, 1)

            def split_u(j):
                dve.wait_ge(u_back, j + 1)
                split_rows(back, u_split[:, :, 0, :], u_split[:, :, 1, :]).then_inc(u_ready, 1)

            def sum_rows(j, i):
                dve.wait_ge(nat_loaded[i % NAT], 32 * j + 16 * (i // NAT + 1))
                V.reduce_sum(row_part[:, i * TB:(i + 1) * TB, bass.ds(j, 1)].rearrange("p t o -> p (t o)"),
                             nat[:, i % NAT], AX.X).then_inc(nat_summed, 1)

            def column(j, first=False, second=False):
                for i in range(NB):
                    if first and i + 1 < NB:
                        make_e(i + 1)
                    if not first:
                        if i == 0:
                            copy_u(j - 1)
                            sum_rows(j - 1, NB - 1)
                            if not second:
                                add_h(j - 2, NB - 1)
                        split_lo(NB * (j - 1) + i, i, i % 2)
                        if i == 0:
                            split_u(j - 1)
                        else:
                            add_h(j - 1, i - 1)
                    if i < NB - 1:
                        sum_rows(j, i)

            make_e(0)
            column(0, first=True)
            column(1, second=True)
            with dve.Fori(2, NB) as j:
                column(j)
            copy_u(NB - 1)
            sum_rows(NB - 1, NB - 1)
            add_h(NB - 2, NB - 1)
            dve.wait_ge(u_back, NB)
            V.tensor_copy(u_last[:, :, :], back).then_inc(u_ready, 1)

            roots = [0]

            def ask_power():
                dve.drain().then_inc(var_ready, 1)
                roots[0] += 1
                return roots[0]

            def over_rows(v):
                return v.unsqueeze(2).broadcast_to([P, TB, F])

            def vec_rows(k):
                return vec[:, k, :].unsqueeze(1).broadcast_to([P, TB, F])

            def rows_of(t, i):
                return t[:, i * TB:(i + 1) * TB]

            def vectors_of(k, i):
                return rows_of(vectors, i)[:, :, k % 2, :]

            def centre(src):
                for t in range(TB):
                    V.bn_stats(stats[:, t, :], src[:, t, :])
                dve.drain()
                for t in range(TB):
                    V.bn_aggr(mean_var[:, t, :], stats[:, t, :])
                dve.drain()
                V.tensor_scalar(power_in[:, :], mean_var[:, :, 1], LN_EPS, None, ALU.add)
                root = ask_power()
                V.tensor_tensor(centred[:, :, :], src[:, :, :], over_rows(mean_var[:, :, 0]), ALU.subtract)
                return root

            def norm(src, dst, meanwhile=None):
                root = centre(src)
                dve.drain()
                if meanwhile is not None:
                    meanwhile()
                dve.wait_ge(pow_ready, root)
                V.tensor_tensor(dst, centred[:, :, :], over_rows(power_out[:, :]), ALU.mult)
                dve.drain()

            def end_l0(i, n, meanwhile=None, soon=None):
                x_i = rows_of(rows, i)
                dve.wait_ge(y_back, n + 1)
                root = centre(yw[n % 2][0])
                dve.drain().then_inc(y_used, 1)
                V.tensor_tensor(tb_[:, :, :], centred[:, :, :], vec_rows(0), ALU.mult)
                V.scalar_tensor_tensor(out=x_i, in0=x_i, scalar=2.0, in1=vec_rows(1), op0=ALU.mult, op1=ALU.add)
                dve.drain()
                dve.wait_ge(pow_ready, root)
                V.tensor_tensor(ta[:, :, :], tb_[:, :, :], over_rows(power_out[:, :]), ALU.mult)
                dve.drain()
                V.tensor_tensor(tb_[:, :, :], ta[:, :, :], x_i, ALU.add)
                dve.drain()
                norm(tb_, vectors_of(0, i), meanwhile)
                dve.drain().then_inc(rows_ready, 1)

            def end_l1(i, n, meanwhile=None, soon=None):
                x_i = vectors_of(0, i)
                V.tensor_scalar(tb_[:, :, :], x_i, 0.9, 1.0, ALU.mult, ALU.add)
                dve.wait_ge(y_back, n + 1)
                V.tensor_tensor(ta[:, :, :], yw[n % 2][0], x_i, ALU.mult)
                dve.drain().then_inc(y_used, 1)
                V.reduce_sum(row_sum[:, :], ta[:, :, :], AX.X)
                dve.drain()
                V.tensor_scalar(row_sum[:, :], row_sum[:, :], 0.01, None, ALU.mult)
                dve.drain()
                V.tensor_tensor(ta[:, :, :], tb_[:, :, :], over_rows(row_sum[:, :]), ALU.subtract)
                dve.drain()
                if soon is not None:
                    soon()
                norm(ta, vectors_of(1, i), meanwhile)
                dve.drain().then_inc(rows_ready, 1)

            def base_l2(i, n):
                dve.wait_ge(xw_ready, n + 1)
                V.tensor_tensor(ta[:, :, :], xw[:, :, F:2 * F], over_rows(rows_of(inv_deg, i)), ALU.mult)
                V.tensor_tensor(tb_[:, :, :], xw[:, :, 0:F], vec_rows(2), ALU.add)
                dve.drain().then_inc(xw_used, 1)
                V.tensor_tensor(rows_of(base, i), ta[:, :, :], tb_[:, :, :], ALU.add)
                dve.drain()

            def end_l2(i, n, meanwhile=None, soon=None):
                x_i = vectors_of(1, i)
                dve.wait_ge(y_back, n + 1)
                V.tensor_tensor(ta[:, :, :], yw[n % 2][0], over_rows(rows_of(inv_deg, i)), ALU.mult)
                dve.drain().then_inc(y_used, 1)
                V.tensor_tensor(tb_[:, :, :], ta[:, :, :], rows_of(base, i), ALU.add)
                dve.drain()
                V.scalar_tensor_tensor(out=ta[:, :, :], in0=tb_[:, :, :], scalar=0.0, in1=tb_[:, :, :],
                                       op0=ALU.max, op1=ALU.mult)
                V.tensor_scalar(tc[:, :, :], tb_[:, :, :], 0.0, None, ALU.max)
                dve.drain()
                if soon is not None:
                    soon()
                V.reduce_sum(row_sum[:, :], ta[:, :, :], AX.X)
                dve.drain()
                V.tensor_scalar(power_in[:, :], row_sum[:, :], L2_EPS * L2_EPS, None, ALU.max)
                root = ask_power()
                if meanwhile is not None:
                    meanwhile()
                dve.wait_ge(pow_ready, root)
                V.tensor_tensor(ta[:, :, :], tc[:, :, :], over_rows(power_out[:, :]), ALU.mult)
                dve.drain()
                V.tensor_tensor(tb_[:, :, :], ta[:, :, :], x_i, ALU.add)
                dve.drain()
                norm(tb_, vectors_of(2, i))
                dve.drain().then_inc(rows_ready, 1)

            def base_l3(i, n):
                dve.wait_ge(xw_ready, n + 1)
                V.tensor_tensor(ta[:, :, :], xw[:, :, 0:F], vec_rows(3), ALU.add)
                dve.drain().then_inc(xw_used, 1)
                V.tensor_tensor(rows_of(base, i), ta[:, :, :], vectors_of(2, i), ALU.add)
                dve.drain()

            def end_t1(i, n, meanwhile=None, soon=None):
                dve.wait_ge(y_back, n + 1)
                V.tensor_copy(vectors_of(3, i), yw[n % 2][0]).then_inc(rows_ready, 1)
                V.tensor_tensor(rows_of(base, i), yw[n % 2][1], rows_of(base, i), ALU.add)
                dve.drain().then_inc(y_used, 1)

            def end_t2(i, n, meanwhile=None, soon=None):
                total = rows_of(base, i)
                dve.wait_ge(y_back, n + 1)
                V.scalar_tensor_tensor(out=vectors_of(4, i), in0=yw[n % 2][0], scalar=2.0, in1=vectors_of(2, i),
                                       op0=ALU.mult, op1=ALU.subtract).then_inc(rows_ready, 1)
                V.scalar_tensor_tensor(out=total, in0=yw[n % 2][1], scalar=2.0, in1=total,
                                       op0=ALU.mult, op1=ALU.add)
                dve.drain().then_inc(y_used, 1)

            def end_l3(i, n, meanwhile=None, soon=None):
                dve.wait_ge(y_back, n + 1)
                V.scalar_tensor_tensor(out=ta[:, :, :], in0=yw[n % 2][0], scalar=2.0, in1=rows_of(base, i),
                                       op0=ALU.mult, op1=ALU.add)
                dve.drain().then_inc(y_used, 1)
                norm(ta, rows_of(rows, i), meanwhile)
                dve.drain().then_inc(out_ready, 1)

            ENDS = (None, end_l1, end_l2, end_t1, end_t2, end_l3)

            def add_last_h(e):
                cols = slice((NB - 1 - e) * BLK, (NB - e) * BLK)
                dve.wait_ge(last_h_done, e + 1)
                V.tensor_tensor(part[:, cols], part[:, cols], ps_h[e % 2][:, :], ALU.add)
                dve.drain().then_inc(hy_ready, 1)

            def add_ahead(e):
                for k in range(1 if e == 0 else e + 2, min(e + 3, NB)):
                    add_last_h(k)

            add_last_h(0)
            dve.wait_ge(weights_loaded, 16 * N_WEIGHTS)
            for e in range(NB):
                end_l0(NB - 1 - e, e, lambda: add_ahead(e))

            V.reduce_sum(inv_deg[:, :], row_part[:, :, :], AX.X)
            V.tensor_tensor(w3x[:, 0, :], w3x[:, 0, :], w3x[:, 1, :], ALU.subtract)
            V.tensor_tensor(twice[:, 1, :], twice[:, 1, :], twice[:, 3, :], ALU.subtract)
            dve.drain()
            V.tensor_scalar(inv_deg[:, :], inv_deg[:, :], 1.0, 1.0, ALU.add, ALU.max)
            dve.drain()
            V.reciprocal(inv_deg[:, :], inv_deg[:, :])
            dve.drain()

            def add_y(s, r):
                i = at(s, r)
                if r <= HEAD[s]:
                    dve.wait_ge(block_done, turn_at[s, 1])
                else:
                    dve.wait_ge(block_done, turn_at[s, r])
                dve.wait_ge(own_copied, NB * s - r)
                cols, parts = slice(i * BLK, (i + 1) * BLK), y_parts(s, r)
                V.tensor_tensor(part[parts, cols], part[parts, cols], ps_both[r % 2][parts, :], ALU.add)\
                    .then_inc(y_added, 1)

            keep_at = {(s, r): b for b, events in after.items() for what, s, r in events if what == "keep"}

            def keep_both(s, r):
                i = at(s, r)
                dve.wait_ge(block_done, keep_at[s, r])
                dve.wait_ge(own_copied, NB * s + r + 1)
                cols, parts = slice(i * BLK, (i + 1) * BLK), half(s)
                V.tensor_tensor(part[parts, cols], part[parts, cols], ps_both[r % 2][parts, :], ALU.add)\
                    .then_inc(kept, 1)

            for b in sorted(after):
                for what, s, r in after[b]:
                    i, n = at(s, r), NB * s + r
                    if what == "keep" and (s, r) in in_both and not (s in SLOW_ENDS and r == NB - 2):
                        keep_both(s, r)
                    if what == "base":
                        (base_l2 if s == 1 else base_l3)(i, n)
                    if what == "turn":
                        early = range(1, HEAD[s] + 1)

                        def first_rows():
                            for k in early:
                                add_y(s, k)

                        if r > 0 and r not in early:
                            add_y(s, r)
                        if r == 0 and s in QUICK_ENDS:
                            ENDS[s](i, n)
                            first_rows()
                        elif r == NB - 1 and s in SLOW_ENDS:
                            ENDS[s](i, n, soon=lambda: keep_both(s, r - 1))
                        else:
                            ENDS[s](i, n, first_rows if r == 0 else None)


_INS = ["x", "adj", "L0_gnn_W_u", "L0_gnn_diag_u", "L0_gnn_par_u", "L0_gnn_W_i", "L0_gnn_diag_i", "L0_gnn_par_i",
        "L0_gnn_ln_gamma", "L0_gnn_ln_beta", "L2_gnn_W", "L2_gnn_b", "L3_gnn_weight", "L3_gnn_bias"]


def kernel(**inputs):
    import numpy as np
    import concourse.bacc as bacc
    from concourse.bass_utils import run_bass_kernel_spmd

    nc = bacc.Bacc("TRN2", target_bir_lowering=False, num_devices=1)
    arrays, args = {}, []
    for name in _INS:
        a = np.ascontiguousarray(inputs[name])
        arrays[f"in_{name}"] = a
        args.append(nc.dram_tensor(f"in_{name}", a.shape, mybir.dt.from_np(a.dtype), kind="ExternalInput").ap())
    out = nc.dram_tensor("out_0", arrays["in_x"].shape, F32, kind="ExternalOutput").ap()
    build(nc, *args, out)
    r = run_bass_kernel_spmd(nc, [arrays], core_ids=[0])
    return r.results[0]["out_0"]
```
